# Optimizing a Trainium2 kernel written in Bass

```python
import numpy as np
import jax
import jax.numpy as jnp

def _softmax(x, axis=-1):
    return jax.nn.softmax(x, axis=axis)

def _gelu(x):
    return jax.nn.gelu(x, approximate=True)

def _silu(x):
    return jax.nn.silu(x)

def _sigmoid(x):
    return jax.nn.sigmoid(x)

def _layernorm(x, axis=-1, eps=1e-05):
    m = jnp.mean(x, axis=axis, keepdims=True)
    v = jnp.var(x, axis=axis, keepdims=True)
    return (x - m) / jnp.sqrt(v + eps)

def _scatter_add(tgt, idx, src, axis=0):
    return tgt.at[idx].add(src)

def _segment_sum(src, seg, n):
    return jax.ops.segment_sum(src, seg, n)
kernel_name = 'mk_gnn_ffn_d1_gnn_r8_9bacb8'

def setup_inputs(seed: int=0):
    np.random.seed(seed)
    _w = jnp.asarray

    def _rec_inputs():
        import jax
        import jax.numpy as jnp
        _gk = jax.random.key(seed)
        x = -0.0003713 + 1 * jax.random.normal(jax.random.fold_in(_gk, 1), (6250, 256), jnp.float32)
        src = jax.random.randint(jax.random.fold_in(_gk, 2), (200000,), 0, 6250, jnp.int32)
        dst = jnp.minimum((6250 * jax.random.uniform(jax.random.fold_in(_gk, 3), (200000,)) ** 2.0).astype(jnp.int32), 49999)
        _o = jnp.argsort(dst, stable=True)
        src = src[_o]
        dst = dst[_o]
        return (x, src, dst)
    x, src, dst = _rec_inputs()

    def _L0_gnn_setup():
        import jax, jax.numpy as jnp
        import numpy as np
        N_NODES = 6250

        def gcn_conv(x, W, b, src, dst, n_nodes):
            h = x @ W
            ones = jnp.ones(src.shape[0], dtype=h.dtype)
            deg = jax.ops.segment_sum(ones, dst, num_segments=n_nodes) + 1.0
            dinv = jax.lax.rsqrt(deg)
            norm = dinv[src] * dinv[dst]
            msg = h[src] * norm[:, None]
            agg = jax.ops.segment_sum(msg, dst, num_segments=n_nodes)
            agg = agg + h * (dinv * dinv)[:, None]
            return agg + b
        key = jax.random.key(seed)
        k1, k2, k3, k4 = jax.random.split(key, 4)
        embedding = jax.random.normal(k1, (N_NODES, 256), dtype=jnp.float32)
        edge_index = jax.random.randint(k2, (2, 100000), 0, N_NODES, dtype=jnp.int64)
        W1 = jax.random.normal(k3, (256, 64), dtype=jnp.float32) / np.sqrt(256.0)
        b1 = jnp.zeros((64,), dtype=jnp.float32)
        W2 = jax.random.normal(k4, (64, 256), dtype=jnp.float32) / np.sqrt(64.0)
        b2 = jnp.zeros((256,), dtype=jnp.float32)
        return {'embedding': embedding, 'edge_index': edge_index, 'W1': W1, 'b1': b1, 'W2': W2, 'b2': b2}
    _L0_gnn_all = _L0_gnn_setup()
    _L0_gnn_in = {k: v for k, v in _L0_gnn_all.items() if k in ('W1', 'b1', 'W2', 'b2')}
    del _L0_gnn_all

    def _L0_ffn_setup():
        import jax, jax.numpy as jnp
        import numpy as np
        B, S, D, H, E, K = (8, 1024, 256, 1024, 8, 2)
        key = jax.random.key(seed)
        ks = jax.random.split(key, 7)
        s_in = 1.0 / np.sqrt(D)
        s_hid = 1.0 / np.sqrt(H)
        return {'x': jax.random.normal(ks[0], (B, S, D), dtype=jnp.float32), 'Wg': jax.random.uniform(ks[1], (E, D), jnp.float32, -s_in, s_in), 'bg': jax.random.uniform(ks[2], (E,), jnp.float32, -s_in, s_in), 'W1': jax.random.uniform(ks[3], (E, H, D), jnp.float32, -s_in, s_in), 'b1': jax.random.uniform(ks[4], (E, H), jnp.float32, -s_in, s_in), 'W2': jax.random.uniform(ks[5], (E, D, H), jnp.float32, -s_hid, s_hid), 'b2': jax.random.uniform(ks[6], (E, D), jnp.float32, -s_hid, s_hid)}
    _L0_ffn_all = _L0_ffn_setup()
    _L0_ffn_in = {k: v for k, v in _L0_ffn_all.items() if k in ('Wg', 'bg', 'W1', 'b1', 'W2', 'b2')}
    del _L0_ffn_all
    return {'x': x, 'src': src, 'dst': dst, 'L0_gnn_W1': _L0_gnn_in['W1'], 'L0_gnn_b1': _L0_gnn_in['b1'], 'L0_gnn_W2': _L0_gnn_in['W2'], 'L0_gnn_b2': _L0_gnn_in['b2'], 'L0_ffn_Wg': _L0_ffn_in['Wg'], 'L0_ffn_bg': _L0_ffn_in['bg'], 'L0_ffn_W1': _L0_ffn_in['W1'], 'L0_ffn_b1': _L0_ffn_in['b1'], 'L0_ffn_W2': _L0_ffn_in['W2'], 'L0_ffn_b2': _L0_ffn_in['b2']}

def reference(x, src, dst, L0_gnn_W1, L0_gnn_b1, L0_gnn_W2, L0_gnn_b2, L0_ffn_Wg, L0_ffn_bg, L0_ffn_W1, L0_ffn_b1, L0_ffn_W2, L0_ffn_b2):
    import jax
    import jax.numpy as jnp

    def _L0_gnn_ref(embedding, edge_index, W1, b1, W2, b2):
        import jax, jax.numpy as jnp
        import numpy as np
        N_NODES = 6250

        def gcn_conv(x, W, b, src, dst, n_nodes):
            h = x @ W
            ones = jnp.ones(src.shape[0], dtype=h.dtype)
            deg = jax.ops.segment_sum(ones, dst, num_segments=n_nodes) + 1.0
            dinv = jax.lax.rsqrt(deg)
            norm = dinv[src] * dinv[dst]
            msg = h[src] * norm[:, None]
            agg = jax.ops.segment_sum(msg, dst, num_segments=n_nodes)
            agg = agg + h * (dinv * dinv)[:, None]
            return agg + b
        src, dst = (edge_index[0], edge_index[1])
        n = embedding.shape[0]
        h1 = jax.nn.relu(gcn_conv(embedding, W1, b1, src, dst, n))
        h2 = jax.nn.relu(gcn_conv(h1, W2, b2, src, dst, n))
        return h2

    def _L0_ffn_ref(x, Wg, bg, W1, b1, W2, b2):
        import jax, jax.numpy as jnp
        import numpy as np
        B, S, D, H, E, K = (8, 1024, 256, 1024, 8, 2)
        gate_scores = jnp.einsum('bsd,ed->bse', x, Wg) + bg
        topk_scores, topk_idx = jax.lax.top_k(gate_scores, K)
        topk_probs = jax.nn.softmax(topk_scores, axis=-1)
        combine = jnp.sum(topk_probs[..., None] * jax.nn.one_hot(topk_idx, E, dtype=x.dtype), axis=-2)
        out = jnp.zeros_like(x)
        for e in range(E):
            h = jax.nn.relu(jnp.einsum('bsd,hd->bsh', x, W1[e]) + b1[e])
            y = jnp.einsum('bsh,dh->bsd', h, W2[e]) + b2[e]
            out = out + combine[..., e:e + 1] * y
        return out
    edge_index = jnp.stack([src, dst])
    x = x + _L0_gnn_ref(_layernorm(x, axis=-1), edge_index, L0_gnn_W1, L0_gnn_b1, L0_gnn_W2, L0_gnn_b2)
    x = x + _L0_ffn_ref(_layernorm(x, axis=-1)[None], L0_ffn_Wg, L0_ffn_bg, L0_ffn_W1, L0_ffn_b1, L0_ffn_W2, L0_ffn_b2)[0]
    return x

_drawn_inputs = setup_inputs


def setup_inputs(seed=0):
    import zlib

    import numpy as np

    out = dict(_drawn_inputs(seed))
    spreads = {'L0_gnn_b1': (0.0, 0.1), 'L0_gnn_b2': (0.0, 0.1)}
    factors = {'L0_ffn_b1': 5.543, 'L0_ffn_b2': 4.371}
    for name, (base, spread) in spreads.items():
        noise = np.random.default_rng([zlib.crc32(name.encode()), seed]).standard_normal(out[name].shape)
        drawn = base * np.exp(spread * noise) if base else spread * noise
        out[name] = jnp.asarray(drawn.astype(out[name].dtype))
    for name, factor in factors.items():
        out[name] = (out[name] * factor).astype(out[name].dtype)
    return out
```

```python
import concourse.bass as bass
from concourse import mybir
from contextlib import ExitStack

F32 = mybir.dt.float32
BF16 = mybir.dt.bfloat16
F16 = mybir.dt.float16
I32 = mybir.dt.int32
ALU = mybir.AluOpType
ACT = mybir.ActivationFunctionType
AX = mybir.AxisListType.X

P = 128
N, D = 6250, 256
F = 64
EDGES = 200000
NE, H = 8, 1024
DK, HB = D // P, H // P
EPS = 1e-5

CH = 125
NCH = N // CH
BC = 5
NPAIR = NCH // BC // 2

TE = 8
GE = TE * P
NCB = -(-N // P)
NCAP = NCB * P

STEPS, SA, SB = 22, 4, 5
NA, NB = STEPS * SA, STEPS * SB
NG = NA + NB
WA, WB = 36, 128
AW = NCAP + WB
KEYS = NCB * WA
PIECES = (13, 12, 12, 12)
UR = 4
FULL_G = EDGES // GE
TAIL_P = (EDGES - FULL_G * GE) // TE
MOST = NCAP // WA + 1
assert sum(PIECES) == NCB and max(PIECES) * WA <= 512 and KEYS <= 2048
assert NG * GE >= EDGES and GE <= 2048
TB = 7
assert NCB % TB == 0

TS = 256
NT = (2 * N + NE * (TS - 1)) // TS
NTP = NT // 2
SHIFT = TS.bit_length() - 1
BIG = 3.0e38
assert NB % 2 == 0 and NA % 2 == 0 and NT % 2 == 0 and N == CH * NCH and NCH == 2 * BC * NPAIR


def gnn_moe(nc, x, src, dst, gW1, gb1, gW2, gb2, Wg, bg, eW1, eb1, eW2, eb2, out):
    table = [nc.dram_tensor(f"table{l}", (NCAP, 3 * F), BF16).ap() for l in range(2)]
    w1t_d = nc.dram_tensor("w1t_d", (P, NE, DK * H), F32).ap()
    w2t_d = nc.dram_tensor("w2t_d", (P, NE, HB * D), F32).ap()
    x2_d = nc.dram_tensor("x2_d", (N, D), F32).ap()
    slots_x = nc.dram_tensor("slots_x", ((NT + 1) * TS, D), F32).ap()
    slots_y = nc.dram_tensor("slots_y", (NT * TS, D), F32).ap()

    ctx = ExitStack()
    with ctx:
        def sb(name, shape, dt=F32):
            return ctx.enter_context(nc.sbuf_tensor(name, shape, dt))

        def sem(name):
            return ctx.enter_context(nc.semaphore(name))

        arena = sb("arena", [P, NE * (DK * H + HB * D)])
        taken = [0]

        def carve(parts, cols):
            a = arena[0:parts, taken[0]:taken[0] + cols]
            taken[0] += cols
            return a

        feat = carve(F + 1, AW)
        deg = carve(F, AW)
        xb = [carve(CH, BC * D).rearrange("p (c d) -> p c d", c=BC) for _ in range(2)]
        rows = [carve(P, TE * 3 * F // 2).bitcast(BF16).rearrange("p (t k f) -> p t k f", t=TE, k=3) for _ in range(2)]
        hot_b = [carve(P, TE * WB // 2).bitcast(BF16).rearrange("p (t w) -> p t w", t=TE) for _ in range(2)]
        dst_i = carve(P, NG * TE).bitcast(I32).rearrange("p (g t) -> p g t", t=TE)
        src_i = carve(P, NG * TE).bitcast(I32).rearrange("p (g t) -> p g t", t=TE)
        dst_f = carve(P, NG * TE).rearrange("p (g t) -> p g t", t=TE)
        key = carve(P, NG * TE).rearrange("p (g t) -> p g t", t=TE)
        src_lo = carve(P, NA * TE).rearrange("p (g t) -> p g t", t=TE)
        src_hi = carve(P, NA * TE).rearrange("p (g t) -> p g t", t=TE)
        span_in = carve(P, 2 * NG)
        span = carve(P, 2 * NG)
        base0 = carve(P, NG)
        base_f = carve(P, NG)
        base_i = carve(P, NG).bitcast(I32)
        in_win = carve(P, NA * TE).rearrange("p (g t) -> p g t", t=TE)
        zeros = carve(P, 2048)
        xnb = [carve(CH, BC * D).rearrange("p (c d) -> p c d", c=BC) for _ in range(2)]
        fchunk = [carve(F + 1, CH) for _ in range(2)]
        assert taken[0] <= NE * (DK * H + HB * D)
        w1t = [arena[:, i * DK * H:(i + 1) * DK * H] for i in range(2)]
        w2t = arena[:, NE * DK * H:NE * (DK * H + HB * D)]

        ones_bf = sb("ones_bf", [P, F], BF16)
        ident = sb("ident", [P, P])
        iota_1 = sb("iota_1", [P, KEYS], F16)
        rest = sb("rest", [P, TB * F])
        lo_s = [sb(f"lo_s{i}", [P, TE]) for i in range(2)]
        key_s = [sb(f"key_s{i}", [P, TE]) for i in range(2)]
        keyb_s = [sb(f"keyb_s{i}", [P, TE]) for i in range(2)]
        widest = sb("widest", [P, 3])
        reached = sb("reached", [P, 2, MOST])
        passes_i = sb("passes_i", [P, 1], I32)
        idx = [sb(f"idx{i}", [P, TE], I32) for i in range(2)]
        gw1 = sb("gw1", [P, DK, F])
        gw2 = sb("gw2", [F + 1, D])
        gb1c = sb("gb1c", [F, 1])
        xT = [sb(f"xT{i}", [P, DK, CH]) for i in range(2)]
        stats = sb("stats", [CH, BC, 6])
        mv = sb("mv", [CH, BC, 2])
        var = sb("var", [CH, BC])
        std = sb("std", [CH, BC])
        rstd = sb("rstd", [CH, BC])
        room = sb("room", [P, NCH * D])
        w1_in = room[:, 0:HB * D].rearrange("p (b d) -> p b d", b=HB)
        w2_in = room[:, 2048:4096].rearrange("p (b h) -> p b h", b=DK)
        w1_out = room[:, 4096:6144]
        w2_out = room[:, 6144:8192]
        counts = room[:, 0:KEYS * SA // 2].bitcast(F16).rearrange("p (b i w) -> p b i w", b=NCB, i=SA)
        at = KEYS * SA // 2
        hot_key = [room[:, at + i * (KEYS // 2):at + (i + 1) * (KEYS // 2)].bitcast(BF16) for i in range(UR)]
        at += UR * (KEYS // 2)
        hot_lo = [room[:, at + i * (P // 2):at + (i + 1) * (P // 2)].bitcast(BF16) for i in range(UR)]
        at += UR * (P // 2)
        parts = room[:, at:at + NCB * 3 * F // 2].bitcast(BF16).rearrange("p (b k f) -> p b k f", b=NCB, k=3)
        assert at + NCB * 3 * F // 2 <= NCH * D
        xn = room[0:CH, :].rearrange("p (c d) -> p c d", d=D)
        tok = [room[:, i * 512:(i + 1) * 512].rearrange("p (h d) -> p h d", h=2) for i in range(2)]
        tokT = [room[:, 1024 + i * 512:1024 + (i + 1) * 512].rearrange("p (k t) -> p k t", k=DK) for i in range(2)]
        hid = room[:, 2048:2048 + HB * TS].rearrange("p (b t) -> p b t", b=HB)
        b2_b = room[:, 5120:5120 + NE * D].rearrange("p (e d) -> p e d", e=NE)
        y = [room[:, 4096 + i * 512:4096 + (i + 1) * 512].rearrange("p (h d) -> p h d", h=2) for i in range(2)]
        wg_in = sb("wg_in", [NE, D])
        wgT = sb("wgT", [P, DK, NE])
        bg_b = sb("bg_b", [CH, NE])
        logit = sb("logit", [CH, NCH, NE])

        def scratch_of(k, cols):
            return arena[:, AW + k:AW + k + cols]

        R = {n: scratch_of(i * NCH * NE, NCH * NE).rearrange("p (c e) -> p c e", e=NE)
             for i, n in enumerate(("a", "first", "second", "sel", "slot"))}
        sums, run = (scratch_of(k * NCH * NE, NCH * NE).rearrange("p (e c) -> p e c", e=NE) for k in (5, 6))
        passed = scratch_of(7 * NCH * NE, (NT + 1) * NE).rearrange("p (t e) -> p t e", e=NE)
        ones_s = sb("ones_s", [P, NE * NCH])
        rev = sb("rev", [P, NE])
        best = [sb(f"best{i}", [P, NCH]) for i in range(2)]
        pick = sb("pick", [P, NCH])
        prob = [sb(f"prob{i}", [P, NCH]) for i in range(2)]
        slot_i = [sb(f"slot_i{i}", [P, NCH], I32) for i in range(2)]
        below = sb("below", [P, P])
        count = sb("count", [P, NE])
        tiles_i = sb("tiles_i", [P, NE], I32)
        tiles_f = sb("tiles_f", [P, NE])
        tile_end = sb("tile_end", [P, NE])
        offset = sb("offset", [P, NE])
        tile_no = sb("tile_no", [P, NT + 1])
        expert_f = sb("expert_f", [P, NT + 1])
        expert_i = sb("expert_i", [P, NT + 1], I32)

        b1_in = sb("b1_in", [NE * HB, P])
        b1c = sb("b1c", [P, NE * HB])

        bank = [ctx.enter_context(nc.psum_tensor(f"bank{i}", [P, 512], F32)) for i in range(8)]

        consts = sem("consts")
        weights_in = sem("weights_in")
        edges_in = sem("edges_in")
        pads_set = sem("pads_set")
        zero_set = sem("zero_set")
        slots_zeroed = sem("slots_zeroed")
        tick = sem("tick")
        small_T = sem("small_T")
        small_copied = sem("small_copied")
        w_in = sem("w_in")
        w_T = sem("w_T")
        w_evac = sem("w_evac")
        w_used = sem("w_used")
        w_stored = sem("w_stored")
        span_ready = sem("span_ready")
        span_reduced = sem("span_reduced")
        passes_ready = sem("passes_ready")
        sqrt_in, sqrt_out = sem("sqrt_in"), sem("sqrt_out")
        scaled = sem("scaled")
        tabT, tabT_copied = sem("tabT"), sem("tabT_copied")
        tab_stored = [sem(f"tab_stored{l}") for l in range(2)]
        agg_done = sem("agg_done")
        relu_in, relu_out = sem("relu_in"), sem("relu_out")
        norm = [{n: sem(f"{n}_{s}") for n in
                 ("var_ready", "std_ready", "xn_ready", "xT_ready", "xT_copied", "mm_ready", "mm_copied", "x2_ready")}
                for s in ("first", "second")]
        x_in = [[sem(f"x_in{s}{i}") for i in range(2)] for s in range(2)]
        x_free = [[sem(f"x_free{s}{i}") for i in range(2)] for s in range(2)]
        z_ready, z_used = sem("z_ready"), sem("z_used")
        x2_stored = [sem(f"x2_stored{i}") for i in range(2)]
        deg_done = {n: [sem(f"{n}_{i}") for i in range(2)] for n in ("deg_mm", "deg_hot", "deg_acc")}
        layer = [{n: sem(f"{n}_{l}") for n in
                  ("hot_a", "used_a", "counted", "evac", "product", "summed", "hot_b", "acc_b")}
                 | {n: [sem(f"{n}_{l}{i}") for i in range(2)] for n in ("gathered", "idx_ready", "done_b")}
                 for l in range(2)]
        logits_done = sem("logits_done")
        exp_in, exp_out = sem("exp_in"), sem("exp_out")
        sel_ready, prefix_ready = sem("sel_ready"), sem("prefix_ready")
        routed = sem("routed")
        scattered = sem("scattered")
        wt_loaded = sem("wt_loaded")
        b2_in = sem("b2_in")
        w1_loaded = [sem(f"w1_loaded{i}") for i in range(2)]
        w1_free = [sem(f"w1_free{i}") for i in range(2)]
        xnb_free = sem("xnb_free")
        f_copied = sem("f_copied")
        tok_in = [sem(f"tok_in{i}") for i in range(2)]
        tokT_ready, tokT_copied = sem("tokT_ready"), sem("tokT_copied")
        hid_ready, hid_copied = sem("hid_ready"), sem("hid_copied")
        y_ready, y_copied = sem("y_ready"), sem("y_copied")
        y_stored = [sem(f"y_stored{i}") for i in range(2)]
        cidx_ready = [sem(f"cidx_ready{i}") for i in range(2)]
        y_gathered = [sem(f"y_gathered{i}") for i in range(2)]
        x2_in = [sem(f"x2_in{i}") for i in range(2)]
        combined = sem("combined")
        out_stored = [sem(f"out_stored{i}") for i in range(2)]

        x_blk = x.rearrange("(b c p) d -> b p c d", c=BC, p=CH)
        x2_blk = x2_d.rearrange("(b c p) d -> b p c d", c=BC, p=CH)
        out_blk = out.rearrange("(b c p) d -> b p c d", c=BC, p=CH)
        sx_t = slots_x.rearrange("(t h p) d -> t p h d", h=2, p=P)
        sy_t = slots_y.rearrange("(t h p) d -> t p h d", h=2, p=P)
        comb = [[arena[0:CH, (3 * i + k) * BC * D:(3 * i + k + 1) * BC * D].rearrange("p (c d) -> p c d", c=BC)
                 for k in range(3)] for i in range(2)]
        cidx = [[sb(f"cidx{i}{k}", [P, BC], I32) for k in range(2)] for i in range(2)]

        def hold(eng, s, value):
            eng.wait_ge(s, value)
            eng.sem_inc(tick, 1)

        block = ctx.enter_context(nc.Block())

        @block.sync
        def _(sp):
            def load_x(s, r, i):
                hold(sp, x_free[s][i], r + 1)
                sp.dma_start(xb[i], x_blk[bass.ds(2 * r + i, 1)].rearrange("o p c d -> (o p) c d")).then_inc(x_in[s][i], 16)

            sp.dma_start(wg_in[:, :], Wg).then_inc(weights_in, 16)
            sp.dma_start(b1_in[:, :], eb1.rearrange("e (b p) -> (e b) p", p=P)).then_inc(weights_in, 16)
            sp.dma_start(gw1[:, :, :], gW1.rearrange("(k p) f -> p k f", p=P)).then_inc(weights_in, 16)
            sp.dma_start(gw2[0:F, :], gW2).then_inc(weights_in, 16)
            sp.dma_start(gw2[F:F + 1, :], gb2.rearrange("(o d) -> o d", o=1)).then_inc(weights_in, 16)
            sp.dma_start(gb1c[:, :], gb1.rearrange("(f o) -> f o", o=1)).then_inc(weights_in, 16)
            sp.dma_start(bg_b[:, :], bg.rearrange("(o e) -> o e", o=1).to_broadcast([CH, NE])).then_inc(weights_in, 16)
            sp.wait_ge(pads_set, 1)
            sp.dma_start(dst_i[:, 0:FULL_G, :], dst[0:FULL_G * GE].rearrange("(g p t) -> p g t", p=P, t=TE)).then_inc(edges_in, 16)
            sp.dma_start(src_i[:, 0:FULL_G, :], src[0:FULL_G * GE].rearrange("(g p t) -> p g t", p=P, t=TE)).then_inc(edges_in, 16)
            sp.dma_start(dst_i[0:TAIL_P, FULL_G, :], dst[FULL_G * GE:EDGES].rearrange("(p t) -> p t", t=TE)).then_inc(edges_in, 16)
            sp.dma_start(src_i[0:TAIL_P, FULL_G, :], src[FULL_G * GE:EDGES].rearrange("(p t) -> p t", t=TE)).then_inc(edges_in, 16)
            with sp.Fori(0, NPAIR) as r:
                for i in range(2):
                    load_x(0, r, i)
            sp.wait_ge(zero_set, 1)
            for k in range((NT + 1) * TS // 1024):
                sp.dma_start(slots_x[k * 1024:(k + 1) * 1024, :].rearrange("(p r) d -> p (r d)", p=P), zeros).then_inc(slots_zeroed, 16)
            rest = (NT + 1) * TS % 1024
            if rest:
                sp.dma_start(slots_x[(NT + 1) * TS - rest:(NT + 1) * TS, :].rearrange("(p r) d -> p (r d)", p=P),
                             zeros[:, 0:rest * D // P]).then_inc(slots_zeroed, 16)
            for l in range(2):
                sp.wait_ge(tabT_copied, (NCB // TB) * (l + 1) + 2)
                sp.dma_start(table[l].rearrange("(c p) f -> p c f", p=P),
                             parts.rearrange("p b k f -> p b (k f)")).then_inc(tab_stored[l], 16)
            for i in range(2):
                sp.sem_inc(x2_stored[i], 1)
            with sp.Fori(0, NPAIR) as r:
                for i in range(2):
                    hold(sp, x2_stored[i], 16 * r + 1)
                    load_x(1, r, i)
                for i in range(2):
                    hold(sp, norm[1]["x2_ready"], 2 * r + i + 1)
                    sp.dma_start(x2_blk[bass.ds(2 * r + i, 1)].rearrange("o p c d -> (o p) c d"), xb[i]).then_inc(x2_stored[i], 16)
            sp.wait_ge(logits_done, 1)
            sp.wait_ge(xnb_free, 2 * NPAIR + 2)
            for i in range(2):
                sp.wait_ge(x2_stored[i], 16 * NPAIR + 1)
            sp.wait_ge(w_stored, 32 * NE + 1)
            sp.wait_ge(slots_zeroed, 16 * -(-(NT + 1) * TS // 1024))
            sp.dma_start(w2t, w2t_d.rearrange("p e c -> p (e c)")).then_inc(wt_loaded, 16)

            sp.wait_ge(routed, 1)

            def load_weights(t, i):
                e = sp.value_load(expert_i[0:1, bass.ds(t, 1)], min_val=0, max_val=NE - 1)
                sp.dma_start(w1t[i], w1t_d[:, bass.ds(e, 1), :].rearrange("p o c -> p (o c)")).then_inc(w1_loaded[i], 16)

            def load_tokens(t, i):
                sp.dma_start(tok[i][:, :, :], sx_t[bass.ds(t, 1)].rearrange("o p h d -> (o p) h d")).then_inc(tok_in[i], 16)

            sp.wait_ge(scattered, 16 * 2 * NCH)
            load_tokens(0, 0)
            for i in range(2):
                sp.sem_inc(w1_free[i], 1)
            load_weights(0, 0)
            sp.dma_start(b2_b, eb2.rearrange("(o e) d -> o e d", o=1).to_broadcast([P, NE, D])).then_inc(b2_in, 16)
            with sp.Fori(0, NTP) as r:
                for i in range(2):
                    hold(sp, w1_free[1 - i], r + 1 + i)
                    load_weights(2 * r + i + 1, 1 - i)
                    hold(sp, tokT_ready, 2 * r + i + 1)
                    load_tokens(2 * r + i + 1, 1 - i)
                    hold(sp, y_copied, 2 * r + i + 3)
                    sp.dma_start(sy_t[bass.ds(2 * r + i, 1)].rearrange("o p h d -> (o p) h d"), y[i][:, :, :]).then_inc(y_stored[i], 16)
            for i in range(2):
                sp.wait_ge(y_stored[i], 16 * NTP + 1)
            with sp.Fori(0, NPAIR) as r:
                for i in range(2):
                    hold(sp, out_stored[i], 16 * r + 1)
                    sp.dma_start(comb[i][2], x2_blk[bass.ds(2 * r + i, 1)].rearrange("o p c d -> (o p) c d")).then_inc(x2_in[i], 16)

        @block.gpsimd
        def _(pool):
            nc.gpsimd.memset(dst_i[:, FULL_G:NG, :], N)
            nc.gpsimd.memset(src_i[:, FULL_G:NG, :], 0)
            pool.drain().then_inc(pads_set, 1)
            nc.gpsimd.memset(ident[:, :], 0.0)
            nc.gpsimd.memset(below[:, :], 1.0)
            nc.gpsimd.memset(ones_bf[:, :], 1.0)
            nc.gpsimd.memset(ones_s[:, :], 1.0)
            nc.gpsimd.iota(iota_1[:, :], [[1, KEYS]], base=1, channel_multiplier=0, allow_small_or_imprecise_dtypes=True)
            nc.gpsimd.iota(rev[:, :], [[-1, NE]], base=NE, channel_multiplier=0, allow_small_or_imprecise_dtypes=True)
            nc.gpsimd.iota(tile_no[:, :], [[1, NT + 1]], base=0, channel_multiplier=0, allow_small_or_imprecise_dtypes=True)
            pool.drain()
            nc.gpsimd.affine_select(out=ident[:, :], in_=ident[:, :], compare_op=ALU.not_equal, fill=1.0, base=0,
                                    pattern=[[-1, P]], channel_multiplier=1)
            nc.gpsimd.affine_select(out=below[:, :], in_=below[:, :], compare_op=ALU.is_gt, fill=0.0, base=0,
                                    pattern=[[1, P]], channel_multiplier=-1)
            pool.drain().then_inc(consts, 1)
            nc.gpsimd.memset(zeros, 0.0).then_inc(zero_set, 1)
            pool.sem_inc(w_used, 1)
            with pool.Fori(0, NE) as e:
                hold(pool, w_used, e + 1)
                pool.dma_start(w1_in, eW1[bass.ds(e, 1)].rearrange("o (b p) d -> p (o b) d", p=P)).then_inc(w_in, 16)
                pool.dma_start(w2_in, eW2[bass.ds(e, 1)].rearrange("o (b p) h -> p (o b) h", p=P)).then_inc(w_in, 16)
            pool.wait_ge(span_ready, 1)
            nc.gpsimd.partition_all_reduce(span[:, :], span_in[:, :], P, bass.bass_isa.ReduceOp.max).then_inc(span_reduced, 1)
            pool.wait_ge(passes_ready, 1)
            pool.wait_ge(edges_in, 64)
            passes = pool.value_load(passes_i[0:1, 0:1], min_val=1, max_val=MOST)
            for l in range(2):
                L = layer[l]
                pool.wait_ge(tab_stored[l], 16)
                with pool.Fori(0, passes) as j:
                    with pool.Fori(0, NB // 2) as g:
                        for i in range(2):
                            r = j * (NB // 2) + g
                            hold(pool, L["done_b"][i], r + 1)
                            nc.gpsimd.tensor_copy(idx[i][:, :], src_i[:, bass.ds(NA + 2 * g + i, 1), :].rearrange("p o t -> p (o t)")).then_inc(L["idx_ready"][i], 1)
                            hold(pool, L["idx_ready"][i], r + 1)
                            for t in range(TE):
                                pool.indirect_dma_start(rows[i][:, t, :, :].rearrange("p k f -> p (k f)"), None, table[l],
                                                        bass.IndirectOffsetOnAxis(ap=idx[i][:, t:t + 1], axis=0)).then_inc(L["gathered"][i], 16)
            pool.wait_ge(routed, 1)
            pool.wait_ge(xnb_free, 2 * NPAIR + 2)
            pool.wait_ge(slots_zeroed, 16 * -(-(NT + 1) * TS // 1024))
            for c in range(NCH):
                for k in range(2):
                    pool.indirect_dma_start(slots_x, bass.IndirectOffsetOnAxis(ap=slot_i[k][0:CH, c:c + 1], axis=0),
                                            xn[:, c, :], None).then_inc(scattered, 16)
            for i in range(2):
                pool.wait_ge(y_stored[i], 16 * NTP + 1)
            with pool.Fori(0, NPAIR) as r:
                for i in range(2):
                    hold(pool, out_stored[i], 16 * r + 1)
                    for k in range(2):
                        nc.gpsimd.tensor_copy(cidx[i][k][0:CH, :], slot_i[k][0:CH, bass.ds((2 * r + i) * BC, BC)]).then_inc(cidx_ready[i], 1)
                    hold(pool, cidx_ready[i], 2 * r + 2)
                    for c in range(BC):
                        for k in range(2):
                            pool.indirect_dma_start(comb[i][k][:, c, :], None, slots_y,
                                                    bass.IndirectOffsetOnAxis(ap=cidx[i][k][0:CH, c:c + 1], axis=0)).then_inc(y_gathered[i], 16)

        @block.vector
        def _(dve):
            V = nc.vector

            def layer_norm(s, i, r, dest):
                q = norm[s]
                for c in range(BC):
                    V.bn_stats(stats[:, c, :], xb[i][:, c, :])
                dve.drain()
                for c in range(BC):
                    V.bn_aggr(mv[:, c, :], stats[:, c, :])
                dve.drain()
                V.tensor_scalar(var[:, :], mv[:, :, 1], EPS, None, ALU.add).then_inc(q["var_ready"], 1)
                hold(dve, q["std_ready"], 2 * r + i + 1)
                V.reciprocal(rstd[:, :], std[:, :])
                dve.drain()
                for c in range(BC):
                    V.tensor_scalar(dest(c), xb[i][:, c, :], mv[:, c, 0:1], rstd[:, c:c + 1], ALU.subtract, ALU.mult)
                dve.drain().then_inc(q["xn_ready"], 1)

            for i in range(2):
                dve.sem_inc(x_free[0][i], 1)
            with dve.Fori(0, NPAIR) as r:
                for i in range(2):
                    hold(dve, x_in[0][i], 16 * r + 16)
                    layer_norm(0, i, r, lambda c: xb[i][:, c, :])
            dve.wait_ge(edges_in, 64)
            V.tensor_copy(dst_f[:, :, :], dst_i[:, :, :])
            scratch = key[:, 0:NA, :].bitcast(I32)
            V.tensor_scalar(scratch, src_i[:, 0:NA, :], P - 1, None, ALU.bitwise_and)
            dve.drain()
            V.tensor_scalar(src_lo, scratch, 1.0, None, ALU.add)
            dve.drain()
            V.tensor_scalar(scratch, src_i[:, 0:NA, :], P.bit_length() - 1, None, ALU.arith_shift_right)
            V.tensor_reduce(base0[:, :], dst_f[:, :, :], AX, ALU.min)
            V.tensor_reduce(span_in[:, NG:2 * NG], dst_f[:, :, :], AX, ALU.max)
            dve.drain()
            V.tensor_scalar(src_hi, scratch, float(WA), None, ALU.mult)
            V.tensor_scalar(span_in[:, 0:NG], base0[:, :], -1.0, None, ALU.mult)
            dve.drain().then_inc(span_ready, 1)
            V.memset(deg, 1.0)
            dve.wait_ge(span_reduced, 1)
            V.tensor_scalar(base0[:, :], span[:, 0:NG], -1.0, None, ALU.mult)
            V.tensor_tensor(base_f[:, :], span[:, 0:NG], span[:, NG:2 * NG], ALU.add)
            dve.drain()
            V.tensor_reduce(widest[:, 0:1], base_f[:, 0:NA], AX, ALU.max)
            V.tensor_reduce(widest[:, 1:2], base_f[:, NA:NG], AX, ALU.max)
            dve.drain()
            for k, w in ((0, WA), (1, WB)):
                V.tensor_scalar(widest[:, k:k + 1], widest[:, k:k + 1], float(w), None, ALU.add)
            dve.drain()
            for k, w in ((0, WA), (1, WB)):
                V.tensor_scalar(reached[:, k, :], iota_1[:, 0:MOST], float(w), widest[:, k:k + 1], ALU.mult, ALU.is_le)
            dve.drain()
            V.tensor_reduce(widest[:, 0:2], reached[:, :, :], AX, ALU.add)
            dve.drain()
            V.tensor_reduce(widest[:, 2:3], widest[:, 0:2], AX, ALU.max)
            dve.drain()
            V.tensor_copy(passes_i[:, :], widest[:, 2:3])
            dve.drain().then_inc(passes_ready, 1)
            passes = dve.value_load(passes_i[0:1, 0:1], min_val=1, max_val=MOST)

            def first_windows():
                V.tensor_copy(base_f[:, :], base0[:, :])
                V.tensor_copy(base_i[:, :], base0[:, :])
                dve.drain()

            def next_windows():
                dve.drain()
                for c, w in ((slice(0, NA), WA), (slice(NA, NG), WB)):
                    V.tensor_scalar(base_f[:, c], base_f[:, c], float(w), float(NCAP), ALU.add, ALU.min)
                dve.drain()
                V.tensor_copy(base_i[:, :], base_f[:, :])
                dve.drain()

            def window_keys():
                V.scalar_tensor_tensor(key, dst_f, 1.0, base_f[:, :].unsqueeze(2).to_broadcast([P, NG, TE]), ALU.add, ALU.subtract)
                dve.drain()

            def pair_keys():
                k = key[:, 0:NA, :]
                V.tensor_scalar(in_win, k, float(WA), None, ALU.is_le)
                dve.drain()
                V.scalar_tensor_tensor(in_win, k, 1.0, in_win, ALU.is_ge, ALU.mult)
                V.tensor_tensor(k, k, src_hi, ALU.add)
                dve.drain()
                V.tensor_tensor(k, k, in_win, ALU.mult)
                dve.drain()

            def degrees(first, groups, width, r0, per_pass, j):
                with dve.Fori(0, groups // 2) as g:
                    r = j * per_pass + r0 + g
                    for i in range(2):
                        hold(dve, deg_done["deg_mm"][i], r + 1)
                        V.tensor_tensor(hot_b[i][:, :, 0:width],
                                        key[:, bass.ds(first + 2 * g + i, 1), :].rearrange("p o t -> p (o t)").unsqueeze(2).to_broadcast([P, TE, width]),
                                        iota_1[:, 0:width].unsqueeze(1).to_broadcast([P, TE, width]),
                                        ALU.is_equal).then_inc(deg_done["deg_hot"][i], 1)
                    for i in range(2):
                        b = dve.value_load(base_i[0:1, bass.ds(first + 2 * g + i, 1)], min_val=0, max_val=NCAP)
                        hold(dve, deg_done["deg_mm"][i], r + 2)
                        dve.drain()
                        V.tensor_tensor(deg[:, bass.ds(b, width)], deg[:, bass.ds(b, width)], bank[i][0:F, 0:width], ALU.add).then_inc(deg_done["deg_acc"][i], 1)

            for i in range(2):
                dve.sem_inc(deg_done["deg_acc"][i], 1)
            first_windows()
            with dve.Fori(0, passes) as j:
                window_keys()
                degrees(0, NA, WA, 0, NG // 2, j)
                degrees(NA, NB, WB, NA // 2, NG // 2, j)
                next_windows()

            def split_table(l):
                if l:
                    dve.wait_ge(tab_stored[0], 16)
                else:
                    dve.wait_ge(w_stored, 32 * NE + 1)
                    dve.sem_inc(tabT_copied, 2)
                for b in range(NCB // TB):
                    dve.wait_ge(tabT, (NCB // TB) * l + b + 1)
                    turned = bank[2 + b % 2][:, 0:TB * F].rearrange("p (b f) -> p b f", f=F)
                    mine = parts[:, b * TB:(b + 1) * TB]
                    left = rest[:, :].rearrange("p (b f) -> p b f", f=F)
                    V.tensor_copy(mine[:, :, 0, :], turned)
                    dve.drain()
                    V.tensor_tensor(left, turned, mine[:, :, 0, :], ALU.subtract)
                    dve.drain()
                    V.tensor_copy(mine[:, :, 1, :], left)
                    dve.drain()
                    V.tensor_tensor(mine[:, :, 2, :], left, mine[:, :, 1, :], ALU.subtract)
                    dve.drain().then_inc(tabT_copied, 1)

            def aggregate(l):
                L = layer[l]
                dve.sem_inc(L["acc_b"], 2)
                dve.sem_inc(L["summed"], 1)
                first_windows()
                with dve.Fori(0, passes) as j:
                    window_keys()
                    pair_keys()
                    with dve.Fori(0, STEPS // 2) as st:
                        turn = j * (STEPS // 2) + st

                        def stage_keys(dest, source, g):
                            V.tensor_copy(dest[:, :], source[:, bass.ds(g, 1), :].rearrange("p o t -> p (o t)"))

                        def hot_a(i):
                            stage_keys(lo_s[i % 2], src_lo, 2 * SA * st + i)
                            stage_keys(key_s[i % 2], key, 2 * SA * st + i)
                            dve.drain()
                            for t in range(TE):
                                u = t % UR
                                hold(dve, L["used_a"], turn * (2 * SA * TE) + i * TE + t + 1)
                                V.tensor_scalar(hot_lo[u], iota_1[:, 0:P], lo_s[i % 2][:, t:t + 1], None, ALU.is_equal)
                                V.tensor_scalar(hot_key[u], iota_1[:, :], key_s[i % 2][:, t:t + 1], None, ALU.is_equal)
                                dve.drain().then_inc(L["hot_a"], 1)

                        def hot_dst(i):
                            stage_keys(keyb_s[i % 2], key, NA + 2 * SB * st + i)
                            dve.drain()
                            for t in range(TE):
                                V.tensor_scalar(hot_b[i % 2][:, t, :], iota_1[:, 0:WB], keyb_s[i % 2][:, t:t + 1], None, ALU.is_equal)
                            dve.drain().then_inc(L["hot_b"], 1)

                        def add_b(i):
                            b = dve.value_load(base_i[0:1, bass.ds(NA + 2 * SB * st + i, 1)], min_val=0, max_val=NCAP)
                            hold(dve, L["done_b"][i % 2], turn * SB + i // 2 + 2)
                            dve.drain()
                            V.tensor_tensor(feat[0:F, bass.ds(b, WB)], feat[0:F, bass.ds(b, WB)], bank[i % 2][0:F, 0:WB], ALU.add).then_inc(L["acc_b"], 1)

                        def add_a(half):
                            hold(dve, L["product"], turn * 2 + half + 1)
                            for i in range(SA):
                                b = dve.value_load(base_i[0:1, bass.ds(2 * SA * st + half * SA + i, 1)], min_val=0, max_val=NCAP)
                                dve.drain()
                                V.tensor_tensor(feat[0:F, bass.ds(b, WA)], feat[0:F, bass.ds(b, WA)],
                                                bank[6][0:F, i * WA:(i + 1) * WA], ALU.add)
                            dve.drain().then_inc(L["summed"], 1)

                        for half in range(2):
                            for i in range(SA):
                                hot_a(half * SA + i)
                                if i:
                                    add_b(half * SB + i - 1)
                                hot_dst(half * SB + i)
                            add_b(half * SB + SA - 1)
                            hot_dst(half * SB + SA)
                            add_a(half)
                            add_b(half * SB + SA)
                    next_windows()

            dve.drain().then_inc(sqrt_in, 1)
            dve.wait_ge(sqrt_out, 1)
            V.reciprocal(deg, deg)
            dve.drain()
            dve.wait_ge(norm[0]["mm_copied"], NCH)
            for l in range(2):
                V.tensor_tensor(feat[0:F, 0:N], feat[0:F, 0:N], deg[:, 0:N], ALU.mult)
                V.memset(feat[0:F, N:AW], 0.0)
                dve.drain().then_inc(scaled, 1)
                split_table(l)
                aggregate(l)
                V.tensor_tensor(feat[0:F, 0:N], feat[0:F, 0:N], deg[:, 0:N], ALU.mult)
                if l == 0:
                    dve.drain().then_inc(relu_in, 1)
                    dve.wait_ge(relu_out, 1)
            V.memset(feat[F:F + 1, 0:N], 1.0)
            dve.drain().then_inc(agg_done, 1)

            for i in range(2):
                dve.sem_inc(x_free[1][i], 1)
            dve.sem_inc(xnb_free, 2)
            with dve.Fori(0, NPAIR) as r:
                for i in range(2):
                    hold(dve, x_in[1][i], 16 * r + 16)
                    hold(dve, xnb_free, 2 * r + i + 1)
                    for c in range(BC):
                        n = BC * i + c
                        hold(dve, z_ready, 2 * BC * r + n + 3)
                        V.scalar_tensor_tensor(xb[i][:, c, :], bank[4 + n % 2][0:CH, 0:D], 0.0, xb[i][:, c, :],
                                               ALU.max, ALU.add).then_inc(z_used, 1)
                    dve.drain().then_inc(norm[1]["x2_ready"], 1)
                    layer_norm(1, i, r, lambda c: xnb[i][:, c, :])
                    dve.sem_inc(x_free[1][i], 1)

            dve.wait_ge(norm[1]["mm_copied"], NCH)
            Q = slice(0, CH)
            V.tensor_tensor(logit[:, :, :], logit[:, :, :], bg_b[:, :].unsqueeze(1).to_broadcast([CH, NCH, NE]), ALU.add)
            V.memset(R["sel"][:, :, :], 0.0)
            dve.drain().then_inc(logits_done, 1)
            a, slot = R["a"], R["slot"]

            def over_e(v):
                return v.unsqueeze(2).to_broadcast([CH, NCH, NE])

            for k, mine in enumerate(("first", "second")):
                V.tensor_reduce(best[k][Q, :], logit[:, :, :], AX, ALU.max)
                dve.drain()
                V.tensor_tensor(a[Q], logit[:, :, :], over_e(best[k][Q, :]), ALU.is_equal)
                dve.drain()
                V.tensor_tensor(a[Q], a[Q], rev[Q, :].unsqueeze(1).to_broadcast([CH, NCH, NE]), ALU.mult)
                dve.drain()
                V.tensor_reduce(pick[Q, :], a[Q], AX, ALU.max)
                dve.drain()
                V.tensor_tensor(R[mine][Q], rev[Q, :].unsqueeze(1).to_broadcast([CH, NCH, NE]), over_e(pick[Q, :]), ALU.is_equal)
                dve.drain()
                if k == 0:
                    V.scalar_tensor_tensor(logit[:, :, :], R[mine][Q], -BIG, logit[:, :, :], ALU.mult, ALU.add)
                V.tensor_tensor(R["sel"][Q], R["sel"][Q], R[mine][Q], ALU.add)
                dve.drain()
            V.tensor_tensor(pick[Q, :], best[1][Q, :], best[0][Q, :], ALU.subtract)
            dve.drain().then_inc(sel_ready, 1)
            dve.wait_ge(exp_out, 1)
            V.tensor_scalar(prob[0][Q, :], prob[1][Q, :], 1.0, None, ALU.add)
            dve.drain()
            V.reciprocal(prob[0][Q, :], prob[0][Q, :])
            dve.drain()
            V.tensor_tensor(prob[1][Q, :], prob[1][Q, :], prob[0][Q, :], ALU.mult)
            dve.wait_ge(prefix_ready, 1)
            V.tensor_copy(sums[:, :, :].rearrange("p e c -> p c e"), bank[6][:, 0:NCH * NE].rearrange("p (c e) -> p c e", e=NE))
            dve.drain()
            V.tensor_tensor_scan(run[:, :, :].rearrange("p e c -> p (e c)"), ones_s[:, :],
                                 sums[:, :, :].rearrange("p e c -> p (e c)"), 0.0, ALU.mult, ALU.add)
            V.tensor_reduce(count[:, :], sums[:, :, :], AX, ALU.add)
            dve.drain()
            V.tensor_scalar(tiles_f[:, :], count[:, :], float(TS - 1), None, ALU.add)
            dve.drain()
            V.tensor_copy(tiles_i[:, :], tiles_f[:, :])
            dve.drain()
            V.tensor_scalar(tiles_i[:, :], tiles_i[:, :], SHIFT, None, ALU.arith_shift_right)
            dve.drain()
            V.tensor_copy(tiles_f[:, :], tiles_i[:, :])
            dve.drain()
            V.tensor_tensor_scan(tile_end[:, :], ones_s[:, 0:NE], tiles_f[:, :], 0.0, ALU.mult, ALU.add)
            V.tensor_tensor(offset[:, :], count[:, :], run[:, :, NCH - 1], ALU.subtract)
            dve.drain()
            V.tensor_tensor(tiles_f[:, :], tile_end[:, :], tiles_f[:, :], ALU.subtract)
            V.tensor_tensor(run[:, :, :], run[:, :, :], sums[:, :, :], ALU.subtract)
            dve.drain()
            V.scalar_tensor_tensor(offset[:, :], tiles_f[:, :], float(TS), offset[:, :], ALU.mult, ALU.add)
            dve.drain()
            V.tensor_tensor(run[:, :, :], run[:, :, :], offset[:, :].unsqueeze(2).to_broadcast([P, NE, NCH]), ALU.add)
            dve.drain()
            V.tensor_tensor(slot[Q], run[Q, :, :].rearrange("p e c -> p c e"),
                            bank[7][Q, 0:NCH * NE].rearrange("p (c e) -> p c e", e=NE), ALU.add)
            V.tensor_tensor(passed[:, :, :], tile_no[:, :].unsqueeze(2).to_broadcast([P, NT + 1, NE]),
                            tile_end[:, :].unsqueeze(1).to_broadcast([P, NT + 1, NE]), ALU.is_ge)
            dve.drain()
            V.tensor_reduce(expert_f[:, :], passed[:, :, :], AX, ALU.add)
            dve.drain()
            V.tensor_scalar(expert_i[:, :], expert_f[:, :], float(NE - 1), None, ALU.min)
            for k, mine in enumerate(("first", "second")):
                V.tensor_tensor(a[Q], slot[Q], R[mine][Q], ALU.mult)
                dve.drain()
                V.tensor_reduce(pick[Q, :], a[Q], AX, ALU.add)
                dve.drain()
                V.tensor_copy(slot_i[k][Q, :], pick[Q, :])
                dve.drain()
            dve.drain().then_inc(routed, 1)

            dve.wait_ge(b2_in, 16)
            dve.sem_inc(y_copied, 2)
            for i in range(2):
                dve.sem_inc(y_stored[i], 1)
            with dve.Fori(0, NTP) as r:
                for i in range(2):
                    e = dve.value_load(expert_i[0:1, bass.ds(2 * r + i, 1)], min_val=0, max_val=NE - 1)
                    hold(dve, y_stored[i], 16 * r + 1)
                    hold(dve, y_ready, 2 * r + i + 1)
                    V.tensor_tensor(y[i][:, :, :], bank[6 + i][:, :].rearrange("p (h d) -> p h d", h=2),
                                    b2_b[:, bass.ds(e, 1), :].to_broadcast([P, 2, D]), ALU.add)
                    dve.drain().then_inc(y_copied, 1)

            for i in range(2):
                dve.sem_inc(out_stored[i], 1)
            with dve.Fori(0, NPAIR) as r:
                for i in range(2):
                    hold(dve, x2_in[i], 16 * r + 16)
                    hold(dve, y_gathered[i], (r + 1) * (32 * BC))
                    for k in range(2):
                        for c in range(BC):
                            V.scalar_tensor_tensor(comb[i][2][:, c, :], comb[i][k][:, c, :],
                                                   prob[k][Q, bass.ds((2 * r + i) * BC + c, 1)],
                                                   comb[i][2][:, c, :], ALU.mult, ALU.add)
                        dve.drain()
                    dve.drain().then_inc(combined, 1)

        @block.scalar
        def _(act):
            A = nc.scalar
            act.wait_ge(small_T, 1)
            A.copy(wgT[:, :, :].rearrange("p k e -> p (k e)"), bank[0][:, 0:DK * NE])
            A.copy(b1c[:, :], bank[1][:, 0:NE * HB])
            act.drain().then_inc(small_copied, 1)
            act.sem_inc(w_evac, 2)
            act.sem_inc(w_stored, 1)
            with act.Fori(0, NE) as e:
                for n in range(8):
                    hold(act, w_T, 8 * e + n + 1)
                    if n == 0:
                        hold(act, w_stored, 32 * e + 1)
                    if n < 4:
                        A.copy(w1_out[:, n * 512:(n + 1) * 512], bank[n % 2][:, :]).then_inc(w_evac, 1)
                    else:
                        A.copy(w2_out[:, (n - 4) * 512:(n - 3) * 512], bank[n % 2][:, :]).then_inc(w_evac, 1)
                act.drain()
                act.dma_start(w1t_d[:, bass.ds(e, 1), :].rearrange("p o c -> p (o c)"), w1_out).then_inc(w_stored, 16)
                act.dma_start(w2t_d[:, bass.ds(e, 1), :].rearrange("p o c -> p (o c)"), w2_out).then_inc(w_stored, 16)

            def norm_side(s, r, i, dest):
                q = norm[s]
                hold(act, q["var_ready"], 2 * r + i + 1)
                A.activation(std[:, :], var[:, :], ACT.Sqrt).then_inc(q["std_ready"], 1)
                for c in range(BC):
                    n = BC * i + c
                    hold(act, q["xT_ready"], 2 * BC * r + n + 1)
                    A.copy(xT[n % 2][:, :, :].rearrange("p k c -> p (k c)"), bank[n % 2][:, 0:DK * CH]).then_inc(q["xT_copied"], 1)
                    hold(act, q["mm_ready"], 2 * BC * r + n + 1)
                    dest(n)

            def h_out(n, r):
                A.copy(feat[0:F, bass.ds((2 * BC * r + n) * CH, CH)], bank[2 + n % 2][0:F, 0:CH]).then_inc(norm[0]["mm_copied"], 1)

            def logit_out(n, r):
                A.copy(logit[:, bass.ds(2 * BC * r + n, 1), :].rearrange("p o e -> p (o e)"), bank[2 + n % 2][0:CH, 0:NE]).then_inc(norm[1]["mm_copied"], 1)

            with act.Fori(0, NPAIR) as r:
                for i in range(2):
                    norm_side(0, r, i, lambda n: h_out(n, r))
                    act.drain().then_inc(x_free[0][i], 1)

            act.wait_ge(sqrt_in, 1)
            A.activation(deg, deg, ACT.Sqrt).then_inc(sqrt_out, 1)

            def counts_out(l):
                L = layer[l]
                act.sem_inc(L["evac"], len(PIECES))
                act.wait_ge(w_stored, 32 * NE + 1)
                with act.Fori(0, act_passes) as j:
                    with act.Fori(0, STEPS) as st:
                        for i in range(SA):
                            b = 0
                            for k, nb in enumerate(PIECES):
                                hold(act, L["counted"], ((j * STEPS + st) * SA + i) * len(PIECES) + k + 1)
                                A.copy(counts[:, b:b + nb, i, :], bank[2 + k][:, 0:nb * WA].rearrange("p (b w) -> p b w", w=WA)).then_inc(L["evac"], 1)
                                b += nb

            act.wait_ge(passes_ready, 1)
            act_passes = act.value_load(passes_i[0:1, 0:1], min_val=1, max_val=MOST)
            counts_out(0)
            act.wait_ge(relu_in, 1)
            A.activation(feat[0:F, 0:N], feat[0:F, 0:N], ACT.Relu, bias=gb1c[:, :]).then_inc(relu_out, 1)
            counts_out(1)
            act.wait_ge(agg_done, 1)
            act.wait_ge(w_stored, 32 * NE + 1)
            act.wait_ge(tab_stored[1], 16)
            act.sem_inc(z_ready, 2)
            with act.Fori(0, NPAIR) as r:
                for i in range(2):
                    for c in range(BC):
                        n = BC * i + c
                        hold(act, z_ready, 2 * BC * r + n + 1)
                        A.copy(fchunk[n % 2], feat[:, bass.ds((2 * BC * r + n) * CH, CH)]).then_inc(f_copied, 1)
                    norm_side(1, r, i, lambda n: logit_out(n, r))
                    A.copy(xn[:, bass.ds((2 * r + i) * BC, BC), :], xnb[i])
                    act.drain().then_inc(xnb_free, 1)
            act.wait_ge(sel_ready, 1)
            A.activation(prob[1][0:CH, :], pick[0:CH, :], ACT.Exp).then_inc(exp_out, 1)

            act.wait_ge(tokT_ready, 1)
            A.copy(tokT[0][:, :, :].rearrange("p k t -> p (k t)"), bank[0][:, :]).then_inc(tokT_copied, 1)
            with act.Fori(0, NTP) as r:
                for i in range(2):
                    e = act.value_load(expert_i[0:1, bass.ds(2 * r + i, 1)], min_val=0, max_val=NE - 1)
                    for b in range(HB):
                        if b % 2 == 0:
                            hold(act, hid_ready, (2 * r + i) * (HB // 2) + b // 2 + 1)
                        A.activation(hid[:, b, :], bank[2 + b // 2][:, (b % 2) * TS:(b % 2 + 1) * TS], ACT.Relu,
                                     bias=b1c[:, bass.ds(e * HB + b, 1)]).then_inc(hid_copied, 1)
                    hold(act, tokT_ready, 2 * r + i + 2)
                    A.copy(tokT[1 - i][:, :, :].rearrange("p k t -> p (k t)"), bank[1 - i][:, :]).then_inc(tokT_copied, 1)

            with act.Fori(0, NPAIR) as r:
                for i in range(2):
                    hold(act, combined, 2 * r + i + 1)
                    act.dma_start(out_blk[bass.ds(2 * r + i, 1)].rearrange("o p c d -> (o p) c d"), comb[i][2]).then_inc(out_stored[i], 16)
            for i in range(2):
                act.wait_ge(out_stored[i], 16 * NPAIR + 1)

        @block.tensor
        def _(pe):
            T = nc.tensor
            pe.wait_ge(consts, 1)
            pe.wait_ge(weights_in, 112)
            for k in range(DK):
                T.transpose(bank[0][:, k * NE:(k + 1) * NE], wg_in[:, k * P:(k + 1) * P], ident[0:NE, 0:NE])
            T.transpose(bank[1][:, 0:NE * HB], b1_in[:, :], ident[0:NE * HB, 0:NE * HB])
            pe.drain().then_inc(small_T, 1)
            pe.wait_ge(small_copied, 1)
            with pe.Fori(0, NE) as e:
                hold(pe, w_in, 32 * e + 32)
                for n in range(8):
                    hold(pe, w_evac, 8 * e + n + 1)
                    for m in range(4):
                        if n < 4:
                            last = T.transpose(bank[n % 2][:, m * P:(m + 1) * P],
                                               w1_in[:, 4 * (n % 2) + m, (n // 2) * P:(n // 2 + 1) * P], ident[:, :])
                        else:
                            f = 4 * (n - 4) + m
                            last = T.transpose(bank[n % 2][:, m * P:(m + 1) * P],
                                               w2_in[:, f % DK, (f // DK) * P:(f // DK + 1) * P], ident[:, :])
                    last.then_inc(w_T, 1)
                pe.drain().then_inc(w_used, 1)
            pe.wait_ge(w_evac, 8 * NE + 2)

            def turn(s, i, c, source):
                n = BC * i + c
                for k in range(DK):
                    T.transpose(bank[n % 2][:, k * CH:(k + 1) * CH], source(k), ident[0:CH, 0:CH])

            with pe.Fori(0, NPAIR) as r:
                q = norm[0]
                for i in range(2):
                    hold(pe, q["xn_ready"], 2 * r + i + 1)
                    for c in range(BC):
                        n = BC * i + c
                        turn(0, i, c, lambda k: xb[i][:, c, k * P:(k + 1) * P])
                        pe.drain().then_inc(q["xT_ready"], 1)
                        hold(pe, q["xT_copied"], 2 * BC * r + n + 1)
                        for k in range(DK):
                            last = T.matmul(bank[2 + n % 2][0:F, 0:CH], gw1[:, k, :], xT[n % 2][:, k, :], start=k == 0, stop=k == DK - 1)
                        last.then_inc(q["mm_ready"], 1)
            pe.wait_ge(norm[0]["mm_copied"], NCH)

            pe.wait_ge(passes_ready, 1)
            passes = pe.value_load(passes_i[0:1, 0:1], min_val=1, max_val=MOST)

            def degrees(groups, width, r0, j):
                with pe.Fori(0, groups // 2) as g:
                    for i in range(2):
                        r = j * (NG // 2) + r0 + g
                        hold(pe, deg_done["deg_hot"][i], r + 1)
                        hold(pe, deg_done["deg_acc"][i], r + 1)
                        for t in range(TE):
                            last = T.matmul(bank[i][0:F, 0:width], ones_bf[:, :], hot_b[i][:, t, 0:width], start=t == 0, stop=t == TE - 1)
                        last.then_inc(deg_done["deg_mm"][i], 1)

            def table_turn(l):
                pe.wait_ge(scaled, l + 1)
                for b in range(NCB // TB):
                    pe.wait_ge(tabT_copied, (NCB // TB) * l + b + 1)
                    for c in range(TB):
                        last = T.transpose(bank[2 + b % 2][:, c * F:(c + 1) * F],
                                           feat[0:F, (TB * b + c) * P:(TB * b + c + 1) * P], ident[0:F, 0:F])
                    last.then_inc(tabT, 1)
                pe.wait_ge(tabT_copied, (NCB // TB) * (l + 1) + 2)

            def aggregate(l):
                L = layer[l]
                pe.sem_inc(L["used_a"], UR)
                for i in range(2):
                    pe.sem_inc(L["done_b"][i], 1)
                with pe.Fori(0, passes) as j:
                    with pe.Fori(0, STEPS // 2) as st:
                        turn = j * (STEPS // 2) + st

                        def count_a(i):
                            for t in range(TE):
                                hold(pe, L["hot_a"], turn * (2 * SA * TE) + i * TE + t + 1)
                                b = 0
                                for k, nb in enumerate(PIECES):
                                    if t == 0:
                                        hold(pe, L["evac"], turn * (2 * SA * len(PIECES)) + i * len(PIECES) + k + 1)
                                    mm = T.matmul(bank[2 + k][:, 0:nb * WA], hot_lo[t % UR], hot_key[t % UR][:, b * WA:(b + nb) * WA],
                                                  start=t == 0, stop=t == TE - 1)
                                    b += nb
                                    if t == TE - 1:
                                        mm.then_inc(L["counted"], 1)
                                if t < TE - 1:
                                    mm.then_inc(L["used_a"], 1)
                            pe.drain().then_inc(L["used_a"], 1)

                        def sum_b(i):
                            s = i % 2
                            hold(pe, L["hot_b"], turn * (2 * SB) + i + 1)
                            hold(pe, L["acc_b"], turn * (2 * SB) + i + 1)
                            hold(pe, L["gathered"][s], (turn * SB + i // 2 + 1) * (16 * TE))
                            for t in range(TE):
                                for k in range(3):
                                    last = T.matmul(bank[s][0:F, 0:WB], rows[s][:, t, k, :], hot_b[s][:, t, :],
                                                    start=t == 0 and k == 0, stop=t == TE - 1 and k == 2)
                            last.then_inc(L["done_b"][s], 1)

                        def product(half):
                            hold(pe, L["evac"], (turn * 2 + half + 1) * (SA * len(PIECES)) + len(PIECES))
                            hold(pe, L["summed"], turn * 2 + half + 1)
                            for b in range(NCB):
                                for k in range(3):
                                    last = T.matmul(bank[6][0:F, 0:SA * WA], parts[:, b, k, :],
                                                    counts[:, b, :, :].rearrange("p i w -> p (i w)"),
                                                    start=b == 0 and k == 0, stop=b == NCB - 1 and k == 2)
                            last.then_inc(L["product"], 1)

                        for half in range(2):
                            for i in range(SA):
                                count_a(half * SA + i)
                                sum_b(half * SB + i)
                            product(half)
                            sum_b(half * SB + SA)

            for i in range(2):
                pe.sem_inc(deg_done["deg_mm"][i], 1)
            with pe.Fori(0, passes) as j:
                degrees(NA, WA, 0, j)
                degrees(NB, WB, NA // 2, j)
            for l in range(2):
                table_turn(l)
                aggregate(l)

            pe.wait_ge(agg_done, 1)
            pe.sem_inc(z_used, 2)
            with pe.Fori(0, NPAIR) as r:
                q = norm[1]
                for i in range(2):
                    for c in range(BC):
                        n = BC * i + c
                        hold(pe, z_used, 2 * BC * r + n + 1)
                        hold(pe, f_copied, 2 * BC * r + n + 1)
                        T.matmul(bank[4 + n % 2][0:CH, 0:D], fchunk[n % 2], gw2[:, :],
                                 start=True, stop=True).then_inc(z_ready, 1)
                    hold(pe, q["xn_ready"], 2 * r + i + 1)
                    for c in range(BC):
                        n = BC * i + c
                        turn(1, i, c, lambda k: xnb[i][:, c, k * P:(k + 1) * P])
                        pe.drain().then_inc(q["xT_ready"], 1)
                        hold(pe, q["xT_copied"], 2 * BC * r + n + 1)
                        for k in range(DK):
                            last = T.matmul(bank[2 + n % 2][0:CH, 0:NE], xT[n % 2][:, k, :], wgT[:, k, :], start=k == 0, stop=k == DK - 1)
                        last.then_inc(q["mm_ready"], 1)

            pe.wait_ge(sel_ready, 1)
            sel = R["sel"][0:CH].rearrange("p c e -> p (c e)")
            T.matmul(bank[6][:, 0:NCH * NE], ones_s[0:CH, 0:P], sel, start=True, stop=True)
            T.matmul(bank[7][0:CH, 0:NCH * NE], below[0:CH, 0:CH], sel, start=True, stop=True).then_inc(prefix_ready, 1)

            def turn_tokens(i):
                for h in range(2):
                    for k in range(DK):
                        last = T.transpose(bank[i][:, k * TS + h * P:k * TS + (h + 1) * P], tok[i][:, h, k * P:(k + 1) * P], ident[:, :])
                last.then_inc(tokT_ready, 1)

            pe.wait_ge(routed, 1)
            pe.wait_ge(wt_loaded, 16)
            pe.wait_ge(tok_in[0], 16)
            turn_tokens(0)
            with pe.Fori(0, NTP) as r:
                for i in range(2):
                    e = pe.value_load(expert_i[0:1, bass.ds(2 * r + i, 1)], min_val=0, max_val=NE - 1)
                    hold(pe, tokT_copied, 2 * r + i + 1)
                    hold(pe, w1_loaded[i], 16 * r + 16)
                    for b in range(HB):
                        for k in range(DK):
                            last = T.matmul(bank[2 + b // 2][:, (b % 2) * TS:(b % 2 + 1) * TS],
                                            w1t[i][:, k * H + b * P:k * H + (b + 1) * P], tokT[i][:, k, :],
                                            start=k == 0, stop=k == DK - 1)
                        if b % 2:
                            last.then_inc(hid_ready, 1)
                    pe.drain().then_inc(w1_free[i], 1)
                    hold(pe, tok_in[1 - i], 16 * r + 16 * (1 + i))
                    turn_tokens(1 - i)
                    hold(pe, hid_copied, (2 * r + i + 1) * HB)
                    hold(pe, y_copied, 2 * r + i + 1)
                    for h in range(2):
                        for b in range(HB):
                            last = T.matmul(bank[6 + i][:, h * D:(h + 1) * D], hid[:, b, h * P:(h + 1) * P],
                                            w2t[:, bass.ds(e * (HB * D) + b * D, D)], start=b == 0, stop=b == HB - 1)
                    last.then_inc(y_ready, 1)


_INS = ['x', 'src', 'dst', 'L0_gnn_W1', 'L0_gnn_b1', 'L0_gnn_W2', 'L0_gnn_b2', 'L0_ffn_Wg', 'L0_ffn_bg',
        'L0_ffn_W1', 'L0_ffn_b1', 'L0_ffn_W2', 'L0_ffn_b2']


def kernel(**inputs):
    import numpy as np
    import concourse.bacc as bacc
    from concourse import mybir as mb
    from concourse.bass_utils import run_bass_kernel_spmd as run

    nc = bacc.Bacc("TRN2", target_bir_lowering=False, num_devices=1)
    arrays, args = {}, []
    for name in _INS:
        a = np.ascontiguousarray(inputs[name])
        arrays[f"in_{name}"] = a
        args.append(nc.dram_tensor(f"in_{name}", a.shape, mb.dt.from_np(a.dtype), kind="ExternalInput").ap())
    o = nc.dram_tensor("out_x", (N, D), mb.dt.float32, kind="ExternalOutput").ap()
    gnn_moe(nc, *args, o)
    r = run(nc, [arrays], core_ids=[0])
    return r.results[0]["out_x"]
```

```python
import concourse.bass as bass
from concourse import mybir
from contextlib import ExitStack

F32 = mybir.dt.float32
BF16 = mybir.dt.bfloat16
F16 = mybir.dt.float16
I32 = mybir.dt.int32
ALU = mybir.AluOpType
ACT = mybir.ActivationFunctionType
AX = mybir.AxisListType.X

P = 128
N, D = 6250, 256
F = 64
EDGES = 200000
NE, H = 8, 1024
DK, HB = D // P, H // P
EPS = 1e-5

CH = 125
NCH = N // CH
BC = 5
NPAIR = NCH // BC // 2

TE = 8
GE = TE * P
NCB = -(-N // P)
NCAP = NCB * P

STEPS, SA, SB = 22, 4, 5
NA, NB = STEPS * SA, STEPS * SB
NG = NA + NB
WA, WB = 32, 72
AW = NCAP + WB
KEYS = NCB * WA
PIECES = (13, 12, 12, 12)
UR = 4
TILES_A = NA * TE + UR
UA, UB = 4, 5
UNITS = NA // UA // 2 + NB // UB // 2
TU = UB * TE
FULL_G = EDGES // GE
TAIL_P = (EDGES - FULL_G * GE) // TE
MOST = NCAP // WA + 1
assert sum(PIECES) == NCB and max(PIECES) * WA <= 512 and KEYS <= 2048
assert NG * GE >= EDGES and GE <= 2048
TB = 7
assert NCB % TB == 0

TS = 256
NT = (2 * N + NE * (TS - 1)) // TS
NTP = NT // 2
SHIFT = TS.bit_length() - 1
BIG = 3.0e38
assert NB % (2 * UB) == 0 and NA % (2 * UA) == 0 and NT % 2 == 0 and N == CH * NCH and NE == 2 * (NPAIR - 1) and NCH == 2 * BC * NPAIR


def gnn_moe(nc, x, src, dst, gW1, gb1, gW2, gb2, Wg, bg, eW1, eb1, eW2, eb2, out):
    table = [nc.dram_tensor(f"table{l}", (NCAP, 3 * F), BF16).ap() for l in range(2)]
    deg_d, dinv_d = (nc.dram_tensor(n, (NCAP,), F32).ap() for n in ("deg_d", "dinv_d"))
    w1t_d = nc.dram_tensor("w1t_d", (P, NE, DK * H), F32).ap()
    w2t_d = nc.dram_tensor("w2t_d", (P, NE, HB * D), F32).ap()
    x2_d = nc.dram_tensor("x2_d", (N, D), F32).ap()
    slots_x = nc.dram_tensor("slots_x", ((NT + 1) * TS, D), F32).ap()
    slots_y = nc.dram_tensor("slots_y", (NT * TS, D), F32).ap()

    ctx = ExitStack()
    with ctx:
        def sb(name, shape, dt=F32):
            return ctx.enter_context(nc.sbuf_tensor(name, shape, dt))

        def sem(name):
            return ctx.enter_context(nc.semaphore(name))

        arena = sb("arena", [P, NE * (DK * H + HB * D)])
        taken = [0]

        def carve(parts, cols):
            a = arena[0:parts, taken[0]:taken[0] + cols]
            taken[0] += cols
            return a

        feat = carve(F + 1, AW)
        deg = carve(F, AW)
        xb = [carve(CH, BC * D).rearrange("p (c d) -> p c d", c=BC) for _ in range(2)]
        rows = [carve(P, TE * 3 * F // 2).bitcast(BF16).rearrange("p (t k f) -> p t k f", t=TE, k=3) for _ in range(2)]
        hot_b = [carve(P, TE * WB // 2).bitcast(BF16).rearrange("p (t w) -> p t w", t=TE) for _ in range(2)]
        dst_i = carve(P, NG * TE).bitcast(I32).rearrange("p (g t) -> p g t", t=TE)
        src_i = carve(P, NG * TE).bitcast(I32).rearrange("p (g t) -> p g t", t=TE)
        dst_f = carve(P, NG * TE).rearrange("p (g t) -> p g t", t=TE)
        key = carve(P, NG * TE).rearrange("p (g t) -> p g t", t=TE)
        src_lo = carve(P, (NA + 1) * TE).rearrange("p (g t) -> p g t", t=TE)
        src_hi = carve(P, NA * TE).rearrange("p (g t) -> p g t", t=TE)
        span_in = carve(P, 2 * NG)
        span = carve(P, 2 * NG)
        base0 = carve(P, NG)
        base_f = carve(P, NG)
        base_i = carve(P, NG).bitcast(I32)
        in_win = carve(P, NA * TE).rearrange("p (g t) -> p g t", t=TE)
        zeros = carve(P, 2048)
        xnb = [carve(CH, BC * D).rearrange("p (c d) -> p c d", c=BC) for _ in range(2)]
        fchunk = [carve(F + 1, CH) for _ in range(2)]
        assert taken[0] <= NE * (DK * H + HB * D)
        w1t = [arena[:, i * DK * H:(i + 1) * DK * H] for i in range(2)]
        w2t = arena[:, NE * DK * H:NE * (DK * H + HB * D)]

        ones_bf = sb("ones_bf", [P, F], BF16)
        ident = sb("ident", [P, P])
        deg_few = sb("deg_few", [NCB, P])
        iota_1 = sb("iota_1", [P, KEYS], F16)
        rest = sb("rest", [P, TB * F])
        lo_s = [sb(f"lo_s{i}", [P, TE], F16) for i in range(2)]
        key_s = [sb(f"key_s{i}", [P, TE]) for i in range(2)]
        keyb_s = [sb(f"keyb_s{i}", [P, TE], F16) for i in range(2)]
        widest = sb("widest", [P, 3])
        reached = sb("reached", [P, 2, MOST])
        passes_i = sb("passes_i", [P, 1], I32)
        idx = [sb(f"idx{i}", [P, SB, TE], I32) for i in range(2)]
        gw1 = sb("gw1", [P, DK, F])
        gw2 = sb("gw2", [F + 1, D])
        gb1c = sb("gb1c", [F, 1])
        xT = [sb(f"xT{i}", [P, DK, CH]) for i in range(2)]
        stats = sb("stats", [CH, BC, 6])
        mv = sb("mv", [CH, BC, 2])
        var = sb("var", [CH, BC])
        std = sb("std", [CH, BC])
        rstd = sb("rstd", [CH, BC])
        room = sb("room", [P, NCH * D])
        w1_in = room[:, 0:HB * D].rearrange("p (b d) -> p b d", b=HB)
        w2_in = room[:, 2048:4096].rearrange("p (b h) -> p b h", b=DK)
        w1_out = room[:, 4096:6144]
        w2_out = room[:, 6144:8192]
        counts = room[:, 0:KEYS * SA // 2].bitcast(F16).rearrange("p (b i w) -> p b i w", b=NCB, i=SA)
        at = KEYS * SA // 2
        hot_key = [room[:, at + i * (KEYS // 2):at + (i + 1) * (KEYS // 2)].bitcast(BF16) for i in range(UR)]
        at += UR * (KEYS // 2)
        hot_lo = [room[:, at + i * (TE * P // 2):at + (i + 1) * (TE * P // 2)].bitcast(BF16).rearrange("p (t n) -> p t n", t=TE) for i in range(2)]
        at += TE * P
        parts = room[:, at:at + NCB * 3 * F // 2].bitcast(BF16).rearrange("p (b k f) -> p b k f", b=NCB, k=3)
        assert at + NCB * 3 * F // 2 <= NCH * D
        hot_deg = [room[:, i * (WB * TU // 2):(i + 1) * (WB * TU // 2)].bitcast(BF16).rearrange("p (w t) -> p w t", w=WB) for i in range(2)]
        iota_t = room[:, 8192:8192 + WB * TU // 2].bitcast(F16).rearrange("p (w t) -> p w t", w=WB)
        key_16 = room[:, 8192 + WB * TU // 2:8192 + (WB * TU + NG * TE) // 2].bitcast(F16)
        xn = room[0:CH, :].rearrange("p (c d) -> p c d", d=D)
        tok = [room[:, i * 512:(i + 1) * 512].rearrange("p (h d) -> p h d", h=2) for i in range(2)]
        tokT = [room[:, 1024 + i * 512:1024 + (i + 1) * 512].rearrange("p (k t) -> p k t", k=DK) for i in range(2)]
        hid = room[:, 2048:2048 + HB * TS].rearrange("p (b t) -> p b t", b=HB)
        b2_b = room[:, 5120:5120 + NE * D].rearrange("p (e d) -> p e d", e=NE)
        y = [room[:, 4096 + i * 512:4096 + (i + 1) * 512].rearrange("p (h d) -> p h d", h=2) for i in range(2)]
        wg_in = sb("wg_in", [NE, D])
        wgT = sb("wgT", [P, DK, NE])
        bg_b = sb("bg_b", [CH, NE])
        logit = sb("logit", [CH, NCH, NE])

        def scratch_of(k, cols):
            return arena[:, AW + k:AW + k + cols]

        R = {n: scratch_of(i * NCH * NE, NCH * NE).rearrange("p (c e) -> p c e", e=NE)
             for i, n in enumerate(("a", "first", "second", "sel", "slot"))}
        sums, run = (scratch_of(k * NCH * NE, NCH * NE).rearrange("p (e c) -> p e c", e=NE) for k in (5, 6))
        passed = scratch_of(7 * NCH * NE, (NT + 1) * NE).rearrange("p (t e) -> p t e", e=NE)
        ones_s = sb("ones_s", [P, NE * NCH])
        rev = sb("rev", [P, NE])
        best = [sb(f"best{i}", [P, NCH]) for i in range(2)]
        pick = sb("pick", [P, NCH])
        prob = [sb(f"prob{i}", [P, NCH]) for i in range(2)]
        slot_i = [sb(f"slot_i{i}", [P, NCH], I32) for i in range(2)]
        below = sb("below", [P, P])
        count = sb("count", [P, NE])
        tiles_i = sb("tiles_i", [P, NE], I32)
        tiles_f = sb("tiles_f", [P, NE])
        tile_end = sb("tile_end", [P, NE])
        offset = sb("offset", [P, NE])
        tile_no = sb("tile_no", [P, NT + 1])
        expert_f = sb("expert_f", [P, NT + 1])
        expert_i = sb("expert_i", [P, NT + 1], I32)

        b1_in = sb("b1_in", [NE * HB, P])
        b1c = sb("b1c", [P, NE * HB])

        bank = [ctx.enter_context(nc.psum_tensor(f"bank{i}", [P, 512], F32)) for i in range(8)]

        consts = sem("consts")
        weights_in = sem("weights_in")
        edges_in = sem("edges_in")
        pads_set = sem("pads_set")
        zero_set = sem("zero_set")
        slots_zeroed = sem("slots_zeroed")
        tick = sem("tick")
        small_T = sem("small_T")
        small_copied = sem("small_copied")
        w_in = [sem(f"w_in{k}") for k in range(2)]
        w_T = sem("w_T")
        w_evac = sem("w_evac")
        w_used = [sem(f"w_used{k}") for k in range(2)]
        w_out = [sem(f"w_out{k}") for k in range(2)]
        span_ready = sem("span_ready")
        span_reduced = sem("span_reduced")
        passes_ready = sem("passes_ready")
        deg_ready, sqrt_out, dinv_ready = sem("deg_ready"), sem("sqrt_out"), sem("dinv_ready")
        deg_stored, deg_in, dinv_stored, dinv_in = (sem(n) for n in ("deg_stored", "deg_in", "dinv_stored", "dinv_in"))
        scaled = sem("scaled")
        tabT, tabT_copied = sem("tabT"), sem("tabT_copied")
        tab_stored = [sem(f"tab_stored{l}") for l in range(2)]
        agg_done = sem("agg_done")
        norm = [{n: sem(f"{n}_{s}") for n in
                 ("var_ready", "std_ready", "xn_ready", "xT_ready", "xT_copied", "mm_ready", "mm_copied", "x2_ready")}
                for s in ("first", "second")]
        x_in = [[sem(f"x_in{s}{i}") for i in range(2)] for s in range(2)]
        x_free = [[sem(f"x_free{s}{i}") for i in range(2)] for s in range(2)]
        z_ready, z_used = sem("z_ready"), sem("z_used")
        x2_stored = [sem(f"x2_stored{i}") for i in range(2)]
        deg_done = {n: [sem(f"{n}_{i}") for i in range(2)] for n in ("deg_mm", "deg_hot", "deg_acc")}
        layer = [{n: sem(f"{n}_{l}") for n in
                  ("hot_a", "used_a", "counted", "evac", "product", "summed", "hot_b", "acc_b", "idx_ready")}
                 | {n: [sem(f"{n}_{l}{i}") for i in range(2)] for n in ("gathered", "done_b")}
                 for l in range(2)]
        logits_done = sem("logits_done")
        exp_in, exp_out = sem("exp_in"), sem("exp_out")
        sel_ready, prefix_ready = sem("sel_ready"), sem("prefix_ready")
        routed = sem("routed")
        scattered = sem("scattered")
        wt_loaded = sem("wt_loaded")
        b2_in = sem("b2_in")
        w1_loaded = [sem(f"w1_loaded{i}") for i in range(2)]
        xnb_turned, xnb_kept = sem("xnb_turned"), sem("xnb_kept")
        f_copied = sem("f_copied")
        tok_in = [sem(f"tok_in{i}") for i in range(2)]
        tokT_ready, tokT_copied = sem("tokT_ready"), sem("tokT_copied")
        hid_ready, hid_copied = sem("hid_ready"), sem("hid_copied")
        y_ready, y_copied = sem("y_ready"), sem("y_copied")
        y_stored = [sem(f"y_stored{i}") for i in range(2)]
        cidx_ready = [sem(f"cidx_ready{i}") for i in range(2)]
        y_gathered = [sem(f"y_gathered{i}") for i in range(2)]
        x2_in = [sem(f"x2_in{i}") for i in range(2)]
        combined = sem("combined")
        out_stored = [sem(f"out_stored{i}") for i in range(2)]

        x_blk = x.rearrange("(b c p) d -> b p c d", c=BC, p=CH)
        x2_blk = x2_d.rearrange("(b c p) d -> b p c d", c=BC, p=CH)
        out_blk = out.rearrange("(b c p) d -> b p c d", c=BC, p=CH)
        sx_t = slots_x.rearrange("(t h p) d -> t p h d", h=2, p=P)
        sy_t = slots_y.rearrange("(t h p) d -> t p h d", h=2, p=P)
        comb = [[arena[0:CH, (3 * i + k) * BC * D:(3 * i + k + 1) * BC * D].rearrange("p (c d) -> p c d", c=BC)
                 for k in range(3)] for i in range(2)]
        cidx = [[sb(f"cidx{i}{k}", [P, BC], I32) for k in range(2)] for i in range(2)]

        def hold(eng, s, value):
            eng.wait_ge(s, value)
            eng.sem_inc(tick, 1)

        block = ctx.enter_context(nc.Block())

        @block.sync
        def _(sp):
            def load_x(s, r, i):
                hold(sp, x_free[s][i], r + 1)
                sp.dma_start(xb[i], x_blk[bass.ds(2 * r + i, 1)].rearrange("o p c d -> (o p) c d")).then_inc(x_in[s][i], 16)

            sp.dma_start(wg_in[:, :], Wg).then_inc(weights_in, 16)
            sp.dma_start(b1_in[:, :], eb1.rearrange("e (b p) -> (e b) p", p=P)).then_inc(weights_in, 16)
            sp.dma_start(gw1[:, :, :], gW1.rearrange("(k p) f -> p k f", p=P)).then_inc(weights_in, 16)
            sp.dma_start(gw2[0:F, :], gW2).then_inc(weights_in, 16)
            sp.dma_start(gw2[F:F + 1, :], gb2.rearrange("(o d) -> o d", o=1)).then_inc(weights_in, 16)
            sp.dma_start(gb1c[:, :], gb1.rearrange("(f o) -> f o", o=1)).then_inc(weights_in, 16)
            sp.dma_start(bg_b[:, :], bg.rearrange("(o e) -> o e", o=1).to_broadcast([CH, NE])).then_inc(weights_in, 16)
            sp.wait_ge(pads_set, 1)
            sp.dma_start(dst_i[:, 0:FULL_G, :], dst[0:FULL_G * GE].rearrange("(g p t) -> p g t", p=P, t=TE)).then_inc(edges_in, 16)
            sp.dma_start(src_i[:, 0:FULL_G, :], src[0:FULL_G * GE].rearrange("(g p t) -> p g t", p=P, t=TE)).then_inc(edges_in, 16)
            sp.dma_start(dst_i[0:TAIL_P, FULL_G, :], dst[FULL_G * GE:EDGES].rearrange("(p t) -> p t", t=TE)).then_inc(edges_in, 16)
            sp.dma_start(src_i[0:TAIL_P, FULL_G, :], src[FULL_G * GE:EDGES].rearrange("(p t) -> p t", t=TE)).then_inc(edges_in, 16)
            with sp.Fori(0, NPAIR) as r:
                for i in range(2):
                    load_x(0, r, i)
            def zero_slots():
                sp.wait_ge(zero_set, 1)
                for k in range((NT + 1) * TS // 1024):
                    sp.dma_start(slots_x[k * 1024:(k + 1) * 1024, :].rearrange("(p r) d -> p (r d)", p=P), zeros).then_inc(slots_zeroed, 16)
                rest = (NT + 1) * TS % 1024
                if rest:
                    sp.dma_start(slots_x[(NT + 1) * TS - rest:(NT + 1) * TS, :].rearrange("(p r) d -> p (r d)", p=P),
                                 zeros[:, 0:rest * D // P]).then_inc(slots_zeroed, 16)

            sp.wait_ge(deg_ready, 1)
            sp.dma_start(deg_d.rearrange("(b p) -> b p", p=P), deg[0:1, 0:NCAP].rearrange("o (b p) -> o b p", p=P)).then_inc(deg_stored, 16)
            sp.wait_ge(deg_stored, 16)
            sp.dma_start(deg_few[:, :], deg_d.rearrange("(b p) -> b p", p=P)).then_inc(deg_in, 16)
            sp.wait_ge(dinv_ready, 1)
            sp.dma_start(dinv_d.rearrange("(b p) -> b p", p=P), deg_few[:, :]).then_inc(dinv_stored, 16)
            sp.wait_ge(dinv_stored, 16)
            sp.dma_start(deg[:, 0:NCAP], dinv_d.rearrange("(o n) -> o n", o=1).to_broadcast([F, NCAP])).then_inc(dinv_in, 16)
            for l in range(2):
                sp.wait_ge(tabT_copied, (NCB // TB) * (l + 1) + 2)
                sp.dma_start(table[l].rearrange("(c p) f -> p c f", p=P),
                             parts.rearrange("p b k f -> p b (k f)")).then_inc(tab_stored[l], 16)
                if l == 0:
                    zero_slots()
            for i in range(2):
                sp.sem_inc(x2_stored[i], 1)
            with sp.Fori(0, NPAIR) as r:
                for i in range(2):
                    hold(sp, x2_stored[i], 16 * r + 1)
                    load_x(1, r, i)
                for i in range(2):
                    hold(sp, norm[1]["x2_ready"], 2 * r + i + 1)
                    sp.dma_start(x2_blk[bass.ds(2 * r + i, 1)].rearrange("o p c d -> (o p) c d"), xb[i]).then_inc(x2_stored[i], 16)
            sp.wait_ge(logits_done, 1)
            sp.wait_ge(xnb_turned, 2 * NPAIR + 2)
            sp.wait_ge(xnb_kept, 2 * NPAIR + 2)
            for i in range(2):
                sp.wait_ge(x2_stored[i], 16 * NPAIR + 1)
            for k in range(2):
                sp.wait_ge(w_out[k], 16 * NE + 1)
            sp.wait_ge(slots_zeroed, 16 * -(-(NT + 1) * TS // 1024))
            sp.dma_start(w2t, w2t_d.rearrange("p e c -> p (e c)")).then_inc(wt_loaded, 16)

            sp.wait_ge(routed, 1)

            def load_weights(t, i):
                e = sp.value_load(expert_i[0:1, bass.ds(t, 1)], min_val=0, max_val=NE - 1)
                sp.dma_start(w1t[i], w1t_d[:, bass.ds(e, 1), :].rearrange("p o c -> p (o c)")).then_inc(w1_loaded[i], 16)

            def load_tokens(t, i):
                sp.dma_start(tok[i][:, :, :], sx_t[bass.ds(t, 1)].rearrange("o p h d -> (o p) h d")).then_inc(tok_in[i], 16)

            sp.wait_ge(scattered, 16 * 2 * NCH)
            load_tokens(0, 0)
            load_weights(0, 0)
            sp.dma_start(b2_b, eb2.rearrange("(o e) d -> o e d", o=1).to_broadcast([P, NE, D])).then_inc(b2_in, 16)
            with sp.Fori(0, NTP) as r:
                for i in range(2):
                    hold(sp, tokT_ready, 2 * r + i + 1)
                    load_tokens(2 * r + i + 1, 1 - i)
                    load_weights(2 * r + i + 1, 1 - i)
                    hold(sp, y_copied, 2 * r + i + 3)
                    sp.dma_start(sy_t[bass.ds(2 * r + i, 1)].rearrange("o p h d -> (o p) h d"), y[i][:, :, :]).then_inc(y_stored[i], 16)
            for i in range(2):
                sp.wait_ge(y_stored[i], 16 * NTP + 1)
            with sp.Fori(0, NPAIR) as r:
                for i in range(2):
                    hold(sp, out_stored[i], 16 * r + 1)
                    sp.dma_start(comb[i][2], x2_blk[bass.ds(2 * r + i, 1)].rearrange("o p c d -> (o p) c d")).then_inc(x2_in[i], 16)

        @block.gpsimd
        def _(pool):
            nc.gpsimd.memset(dst_i[:, FULL_G:NG, :], N)
            nc.gpsimd.memset(src_i[:, FULL_G:NG, :], 0)
            pool.drain().then_inc(pads_set, 1)
            nc.gpsimd.memset(ident[:, :], 0.0)
            nc.gpsimd.memset(below[:, :], 1.0)
            nc.gpsimd.memset(ones_bf[:, :], 1.0)
            nc.gpsimd.memset(ones_s[:, :], 1.0)
            nc.gpsimd.iota(iota_1[:, :], [[1, KEYS]], base=1, channel_multiplier=0, allow_small_or_imprecise_dtypes=True)
            nc.gpsimd.iota(iota_t, [[1, WB], [0, TU]], base=1, channel_multiplier=0, allow_small_or_imprecise_dtypes=True)
            nc.gpsimd.iota(rev[:, :], [[-1, NE]], base=NE, channel_multiplier=0, allow_small_or_imprecise_dtypes=True)
            nc.gpsimd.iota(tile_no[:, :], [[1, NT + 1]], base=0, channel_multiplier=0, allow_small_or_imprecise_dtypes=True)
            pool.drain()
            nc.gpsimd.affine_select(out=ident[:, :], in_=ident[:, :], compare_op=ALU.not_equal, fill=1.0, base=0,
                                    pattern=[[-1, P]], channel_multiplier=1)
            nc.gpsimd.affine_select(out=below[:, :], in_=below[:, :], compare_op=ALU.is_gt, fill=0.0, base=0,
                                    pattern=[[1, P]], channel_multiplier=-1)
            pool.drain().then_inc(consts, 1)
            nc.gpsimd.memset(zeros, 0.0).then_inc(zero_set, 1)
            def load_expert(e, k):
                w, stage = ((eW1, w1_in), (eW2, w2_in))[k]
                pool.dma_start(stage, w[bass.ds(e, 1)].rearrange("o (b p) c -> p (o b) c", p=P)).then_inc(w_in[k], 16)

            for k in range(2):
                load_expert(0, k)
            with pool.Fori(1, NE) as e:
                for k in range(2):
                    hold(pool, w_used[k], e)
                    load_expert(e, k)
            pool.wait_ge(span_ready, 1)
            nc.gpsimd.partition_all_reduce(span[:, :], span_in[:, :], P, bass.bass_isa.ReduceOp.max).then_inc(span_reduced, 1)
            pool.wait_ge(passes_ready, 1)
            pool.wait_ge(edges_in, 64)
            passes = pool.value_load(passes_i[0:1, 0:1], min_val=1, max_val=MOST)
            for l in range(2):
                L = layer[l]
                pool.wait_ge(tab_stored[l], 16)
                with pool.Fori(0, passes) as j:
                    with pool.Fori(0, STEPS // 2) as st:
                        turn = j * (STEPS // 2) + st
                        for half in range(2):
                            nc.gpsimd.tensor_copy(idx[half][:, :, :], src_i[:, bass.ds(NA + (2 * st + half) * SB, SB), :]).then_inc(L["idx_ready"], 1)
                            hold(pool, L["idx_ready"], 2 * turn + half + 1)
                            for i in range(SB):
                                n = half * SB + i
                                hold(pool, L["done_b"][n % 2], turn * SB + n // 2 + 1)
                                for t in range(TE):
                                    pool.indirect_dma_start(rows[n % 2][:, t, :, :].rearrange("p k f -> p (k f)"), None, table[l],
                                                            bass.IndirectOffsetOnAxis(ap=idx[half][:, i, t:t + 1], axis=0)).then_inc(L["gathered"][n % 2], 16)
            pool.wait_ge(agg_done, 1)
            with pool.Fori(0, NPAIR) as r:
                for i in range(2):
                    hold(pool, norm[1]["xn_ready"], 2 * r + i + 1)
                    nc.gpsimd.tensor_copy(xn[:, bass.ds((2 * r + i) * BC, BC), :], xnb[i]).then_inc(xnb_kept, 1)
            pool.wait_ge(routed, 1)
            pool.wait_ge(xnb_kept, 2 * NPAIR + 2)
            pool.wait_ge(slots_zeroed, 16 * -(-(NT + 1) * TS // 1024))
            for c in range(NCH):
                for k in range(2):
                    pool.indirect_dma_start(slots_x, bass.IndirectOffsetOnAxis(ap=slot_i[k][0:CH, c:c + 1], axis=0),
                                            xn[:, c, :], None).then_inc(scattered, 16)
            for i in range(2):
                pool.wait_ge(y_stored[i], 16 * NTP + 1)
            with pool.Fori(0, NPAIR) as r:
                for i in range(2):
                    hold(pool, out_stored[i], 16 * r + 1)
                    for k in range(2):
                        nc.gpsimd.tensor_copy(cidx[i][k][0:CH, :], slot_i[k][0:CH, bass.ds((2 * r + i) * BC, BC)]).then_inc(cidx_ready[i], 1)
                    hold(pool, cidx_ready[i], 2 * r + 2)
                    for c in range(BC):
                        for k in range(2):
                            pool.indirect_dma_start(comb[i][k][:, c, :], None, slots_y,
                                                    bass.IndirectOffsetOnAxis(ap=cidx[i][k][0:CH, c:c + 1], axis=0)).then_inc(y_gathered[i], 16)

        @block.vector
        def _(dve):
            V = nc.vector

            def layer_norm(s, i, r, dest):
                q = norm[s]
                for c in range(BC):
                    V.bn_stats(stats[:, c, :], xb[i][:, c, :])
                dve.drain()
                for c in range(BC):
                    V.bn_aggr(mv[:, c, :], stats[:, c, :])
                dve.drain()
                V.tensor_scalar(var[:, :], mv[:, :, 1], EPS, None, ALU.add).then_inc(q["var_ready"], 1)
                hold(dve, q["std_ready"], 2 * r + i + 1)
                V.reciprocal(rstd[:, :], std[:, :])
                dve.drain()
                for c in range(BC):
                    V.tensor_scalar(dest(c), xb[i][:, c, :], mv[:, c, 0:1], rstd[:, c:c + 1], ALU.subtract, ALU.mult)
                dve.drain().then_inc(q["xn_ready"], 1)

            for i in range(2):
                dve.sem_inc(x_free[0][i], 1)
            with dve.Fori(0, NPAIR) as r:
                for i in range(2):
                    hold(dve, x_in[0][i], 16 * r + 16)
                    layer_norm(0, i, r, lambda c: xb[i][:, c, :])
            dve.wait_ge(edges_in, 64)
            V.tensor_copy(dst_f[:, :, :], dst_i[:, :, :])
            scratch = key[:, 0:NA, :].bitcast(I32)
            V.tensor_scalar(scratch, src_i[:, 0:NA, :], P - 1, None, ALU.bitwise_and)
            dve.drain()
            V.tensor_scalar(src_lo[:, 0:NA, :], scratch, 1.0, None, ALU.add)
            V.memset(src_lo[:, NA, :], 0.0)
            dve.drain()
            V.tensor_scalar(scratch, src_i[:, 0:NA, :], P.bit_length() - 1, None, ALU.arith_shift_right)
            V.tensor_reduce(base0[:, :], dst_f[:, :, :], AX, ALU.min)
            V.tensor_reduce(span_in[:, NG:2 * NG], dst_f[:, :, :], AX, ALU.max)
            dve.drain()
            V.tensor_scalar(src_hi, scratch, float(WA), None, ALU.mult)
            V.tensor_scalar(span_in[:, 0:NG], base0[:, :], -1.0, None, ALU.mult)
            dve.drain().then_inc(span_ready, 1)
            V.memset(deg, 1.0)
            dve.wait_ge(span_reduced, 1)
            V.tensor_scalar(base0[:, :], span[:, 0:NG], -1.0, None, ALU.mult)
            V.tensor_tensor(base_f[:, :], span[:, 0:NG], span[:, NG:2 * NG], ALU.add)
            dve.drain()
            V.tensor_reduce(widest[:, 0:1], base_f[:, 0:NA], AX, ALU.max)
            V.tensor_reduce(widest[:, 1:2], base_f[:, NA:NG], AX, ALU.max)
            dve.drain()
            for k, w in ((0, WA), (1, WB)):
                V.tensor_scalar(widest[:, k:k + 1], widest[:, k:k + 1], float(w), None, ALU.add)
            dve.drain()
            for k, w in ((0, WA), (1, WB)):
                V.tensor_scalar(reached[:, k, :], iota_1[:, 0:MOST], float(w), widest[:, k:k + 1], ALU.mult, ALU.is_le)
            dve.drain()
            V.tensor_reduce(widest[:, 0:2], reached[:, :, :], AX, ALU.add)
            dve.drain()
            V.tensor_reduce(widest[:, 2:3], widest[:, 0:2], AX, ALU.max)
            dve.drain()
            V.tensor_copy(passes_i[:, :], widest[:, 2:3])
            dve.drain().then_inc(passes_ready, 1)
            passes = dve.value_load(passes_i[0:1, 0:1], min_val=1, max_val=MOST)

            def first_windows():
                V.tensor_copy(base_f[:, :], base0[:, :])
                V.tensor_copy(base_i[:, :], base0[:, :])
                dve.drain()

            def next_windows():
                dve.drain()
                for c, w in ((slice(0, NA), WA), (slice(NA, NG), WB)):
                    V.tensor_scalar(base_f[:, c], base_f[:, c], float(w), float(NCAP), ALU.add, ALU.min)
                dve.drain()
                V.tensor_copy(base_i[:, :], base_f[:, :])
                dve.drain()

            def window_keys():
                V.scalar_tensor_tensor(key, dst_f, 1.0, base_f[:, :].unsqueeze(2).to_broadcast([P, NG, TE]), ALU.add, ALU.subtract)
                dve.drain()

            def pair_keys():
                k = key[:, 0:NA, :]
                V.tensor_scalar(in_win, k, float(WA), None, ALU.is_le)
                dve.drain()
                V.scalar_tensor_tensor(in_win, k, 1.0, in_win, ALU.is_ge, ALU.mult)
                V.tensor_tensor(k, k, src_hi, ALU.add)
                dve.drain()
                V.tensor_tensor(k, k, in_win, ALU.mult)
                dve.drain()

            def degrees(j, first, units, size, width, r0):
                with dve.Fori(0, units // 2) as g:
                    r = j * UNITS + r0 + g
                    for i in range(2):
                        tiles = size * TE
                        hold(dve, deg_done["deg_mm"][i], r + 1)
                        V.tensor_tensor(hot_deg[i][:, 0:width, 0:tiles],
                                        key_16[:, bass.ds((first + (2 * g + i) * size) * TE, tiles)].unsqueeze(1).to_broadcast([P, width, tiles]),
                                        iota_t[:, 0:width, 0:tiles], ALU.is_equal).then_inc(deg_done["deg_hot"][i], 1)
                    for i in range(2):
                        starts = [dve.value_load(base_i[0:1, bass.ds(first + (2 * g + i) * size + m, 1)], min_val=0, max_val=NCAP)
                                  for m in range(size)]
                        hold(dve, deg_done["deg_mm"][i], r + 2)
                        for m, b in enumerate(starts):
                            dve.drain()
                            V.tensor_tensor(deg[:, bass.ds(b, width)], deg[:, bass.ds(b, width)],
                                            bank[2 * i + m // 4][0:F, (m % 4) * width:(m % 4 + 1) * width], ALU.add)
                        dve.drain().then_inc(deg_done["deg_acc"][i], 1)

            for i in range(2):
                dve.sem_inc(deg_done["deg_acc"][i], 1)
            for k in range(2):
                dve.wait_ge(w_out[k], 16 * NE + 1)
            first_windows()
            with dve.Fori(0, passes) as j:
                window_keys()
                V.tensor_copy(key_16, key.rearrange("p g t -> p (g t)"))
                dve.drain()
                degrees(j, 0, NA // UA, UA, WA, 0)
                degrees(j, NA, NB // UB, UB, WB, NA // UA // 2)
                next_windows()

            def scale_and_split(l):
                if l == 0:
                    dve.sem_inc(tabT_copied, 2)
                for b in range(NCB // TB + 1):
                    if b < NCB // TB:
                        c = slice(b * TB * P, min((b + 1) * TB * P, N))
                        V.tensor_tensor(feat[0:F, c], feat[0:F, c], deg[:, c], ALU.mult)
                        if l:
                            dve.drain()
                            V.tensor_scalar(feat[0:F, c], feat[0:F, c], gb1c[:, :], 0.0, ALU.add, ALU.max)
                            dve.drain()
                            V.tensor_tensor(feat[0:F, c], feat[0:F, c], deg[:, c], ALU.mult)
                        dve.drain().then_inc(scaled, 1)
                    if b:
                        m = b - 1
                        dve.wait_ge(tabT, (NCB // TB) * l + m + 1)
                        turned = bank[2 + m % 2][:, 0:TB * F].rearrange("p (b f) -> p b f", f=F)
                        mine = parts[:, m * TB:(m + 1) * TB]
                        left = rest[:, :].rearrange("p (b f) -> p b f", f=F)
                        V.tensor_copy(mine[:, :, 0, :], turned)
                        dve.drain()
                        V.tensor_tensor(left, turned, mine[:, :, 0, :], ALU.subtract)
                        dve.drain()
                        V.tensor_copy(mine[:, :, 1, :], left)
                        dve.drain()
                        V.tensor_tensor(mine[:, :, 2, :], left, mine[:, :, 1, :], ALU.subtract)
                        dve.drain().then_inc(tabT_copied, 1)

            def stage_keys(dest, source, g):
                V.tensor_copy(dest[:, :], source[:, bass.ds(g, 1), :].rearrange("p o t -> p (o t)"))

            def one_hot(out, keys, width):
                return V.tensor_tensor(out, keys[:, :].unsqueeze(2).to_broadcast([P, TE, width]),
                                       iota_1[:, 0:width].unsqueeze(1).to_broadcast([P, TE, width]), ALU.is_equal)

            def aggregate(l):
                L = layer[l]
                dve.sem_inc(L["acc_b"], 2)
                dve.sem_inc(L["summed"], 1)
                first_windows()
                with dve.Fori(0, passes) as j:
                    window_keys()
                    pair_keys()
                    stage_keys(lo_s[0], src_lo, 0)
                    stage_keys(key_s[0], key, 0)
                    dve.drain()
                    one_hot(hot_lo[0], lo_s[0], P)
                    for t in range(UR):
                        dve.wait_ge(L["used_a"], j * TILES_A + t + 1)
                        V.tensor_scalar(hot_key[t], iota_1[:, :], key_s[0][:, t:t + 1], None, ALU.is_equal).then_inc(L["hot_a"], 1)
                    with dve.Fori(0, STEPS // 2) as st:
                        turn = j * (STEPS // 2) + st

                        def hot_a(i, tiles):
                            if tiles[0] == 0:
                                stage_keys(lo_s[i % 2], src_lo, 2 * SA * st + i)
                                stage_keys(key_s[i % 2], key, 2 * SA * st + i)
                                dve.drain()
                                one_hot(hot_lo[i % 2], lo_s[i % 2], P)
                            for t in tiles:
                                dve.wait_ge(L["used_a"], st * (2 * SA * TE) + j * TILES_A + i * TE + t + 1)
                                V.tensor_scalar(hot_key[t % UR], iota_1[:, :], key_s[i % 2][:, t:t + 1], None, ALU.is_equal).then_inc(L["hot_a"], 1)

                        def hot_dst(i):
                            stage_keys(keyb_s[i % 2], key, NA + 2 * SB * st + i)
                            dve.drain()
                            one_hot(hot_b[i % 2], keyb_s[i % 2], WB).then_inc(L["hot_b"], 1)

                        def add_b(i):
                            b = dve.value_load(base_i[0:1, bass.ds(NA + 2 * SB * st + i, 1)], min_val=0, max_val=NCAP)
                            hold(dve, L["done_b"][i % 2], turn * SB + i // 2 + 2)
                            dve.drain()
                            V.tensor_tensor(feat[0:F, bass.ds(b, WB)], feat[0:F, bass.ds(b, WB)], bank[i % 2][0:F, 0:WB], ALU.add).then_inc(L["acc_b"], 1)

                        def add_a(half):
                            starts = [dve.value_load(base_i[0:1, bass.ds(2 * SA * st + half * SA + i, 1)], min_val=0, max_val=NCAP)
                                      for i in range(SA)]
                            hold(dve, L["product"], turn * 2 + half + 1)
                            for i, b in enumerate(starts):
                                dve.drain()
                                V.tensor_tensor(feat[0:F, bass.ds(b, WA)], feat[0:F, bass.ds(b, WA)],
                                                bank[6][0:F, i * WA:(i + 1) * WA], ALU.add)
                            dve.drain().then_inc(L["summed"], 1)

                        for half in range(2):
                            for i in range(SA):
                                hot_a(half * SA + i, range(UR, TE) if i == 0 else range(TE))
                                if i:
                                    add_b(half * SB + i - 1)
                                hot_dst(half * SB + i)
                            add_b(half * SB + SA - 1)
                            hot_dst(half * SB + SA)
                            hot_a((half + 1) * SA, range(UR))
                            add_a(half)
                            add_b(half * SB + SA)
                    next_windows()

            dve.drain().then_inc(deg_ready, 1)
            dve.wait_ge(sqrt_out, 1)
            V.reciprocal(deg_few[:, :], deg_few[:, :])
            dve.drain().then_inc(dinv_ready, 1)
            dve.wait_ge(dinv_in, 16)
            dve.wait_ge(norm[0]["mm_copied"], NCH)
            for l in range(2):
                V.memset(feat[0:F, N:AW], 0.0)
                if l:
                    dve.wait_ge(tab_stored[0], 16)
                scale_and_split(l)
                aggregate(l)
            V.tensor_tensor(feat[0:F, 0:N], feat[0:F, 0:N], deg[:, 0:N], ALU.mult)
            V.memset(feat[F:F + 1, 0:N], 1.0)
            dve.drain().then_inc(agg_done, 1)

            for i in range(2):
                dve.sem_inc(x_free[1][i], 1)
            dve.sem_inc(xnb_turned, 2)
            dve.sem_inc(xnb_kept, 2)
            with dve.Fori(0, NPAIR) as r:
                for i in range(2):
                    hold(dve, x_in[1][i], 16 * r + 16)
                    hold(dve, xnb_turned, 2 * r + i + 1)
                    hold(dve, xnb_kept, 2 * r + i + 1)
                    for c in range(BC):
                        n = BC * i + c
                        hold(dve, z_ready, 2 * BC * r + n + 3)
                        V.scalar_tensor_tensor(xb[i][:, c, :], bank[4 + n % 2][0:CH, 0:D], 0.0, xb[i][:, c, :],
                                               ALU.max, ALU.add).then_inc(z_used, 1)
                    dve.drain().then_inc(norm[1]["x2_ready"], 1)
                    layer_norm(1, i, r, lambda c: xnb[i][:, c, :])
                    dve.sem_inc(x_free[1][i], 1)

            dve.wait_ge(norm[1]["mm_copied"], NCH)
            Q = slice(0, CH)
            V.tensor_tensor(logit[:, :, :], logit[:, :, :], bg_b[:, :].unsqueeze(1).to_broadcast([CH, NCH, NE]), ALU.add)
            V.memset(R["sel"][:, :, :], 0.0)
            dve.drain().then_inc(logits_done, 1)
            a, slot = R["a"], R["slot"]

            def over_e(v):
                return v.unsqueeze(2).to_broadcast([CH, NCH, NE])

            for k, mine in enumerate(("first", "second")):
                V.tensor_reduce(best[k][Q, :], logit[:, :, :], AX, ALU.max)
                dve.drain()
                V.tensor_tensor(a[Q], logit[:, :, :], over_e(best[k][Q, :]), ALU.is_equal)
                dve.drain()
                V.tensor_tensor(a[Q], a[Q], rev[Q, :].unsqueeze(1).to_broadcast([CH, NCH, NE]), ALU.mult)
                dve.drain()
                V.tensor_reduce(pick[Q, :], a[Q], AX, ALU.max)
                dve.drain()
                V.tensor_tensor(R[mine][Q], rev[Q, :].unsqueeze(1).to_broadcast([CH, NCH, NE]), over_e(pick[Q, :]), ALU.is_equal)
                dve.drain()
                if k == 0:
                    V.scalar_tensor_tensor(logit[:, :, :], R[mine][Q], -BIG, logit[:, :, :], ALU.mult, ALU.add)
                V.tensor_tensor(R["sel"][Q], R["sel"][Q], R[mine][Q], ALU.add)
                dve.drain()
            V.tensor_tensor(pick[Q, :], best[1][Q, :], best[0][Q, :], ALU.subtract)
            dve.drain().then_inc(sel_ready, 1)
            dve.wait_ge(exp_out, 1)
            V.tensor_scalar(prob[0][Q, :], prob[1][Q, :], 1.0, None, ALU.add)
            dve.drain()
            V.reciprocal(prob[0][Q, :], prob[0][Q, :])
            dve.drain()
            V.tensor_tensor(prob[1][Q, :], prob[1][Q, :], prob[0][Q, :], ALU.mult)
            dve.wait_ge(prefix_ready, 1)
            V.tensor_copy(sums[:, :, :].rearrange("p e c -> p c e"), bank[6][:, 0:NCH * NE].rearrange("p (c e) -> p c e", e=NE))
            dve.drain()
            V.tensor_tensor_scan(run[:, :, :].rearrange("p e c -> p (e c)"), ones_s[:, :],
                                 sums[:, :, :].rearrange("p e c -> p (e c)"), 0.0, ALU.mult, ALU.add)
            V.tensor_reduce(count[:, :], sums[:, :, :], AX, ALU.add)
            dve.drain()
            V.tensor_scalar(tiles_f[:, :], count[:, :], float(TS - 1), None, ALU.add)
            dve.drain()
            V.tensor_copy(tiles_i[:, :], tiles_f[:, :])
            dve.drain()
            V.tensor_scalar(tiles_i[:, :], tiles_i[:, :], SHIFT, None, ALU.arith_shift_right)
            dve.drain()
            V.tensor_copy(tiles_f[:, :], tiles_i[:, :])
            dve.drain()
            V.tensor_tensor_scan(tile_end[:, :], ones_s[:, 0:NE], tiles_f[:, :], 0.0, ALU.mult, ALU.add)
            V.tensor_tensor(offset[:, :], count[:, :], run[:, :, NCH - 1], ALU.subtract)
            dve.drain()
            V.tensor_tensor(tiles_f[:, :], tile_end[:, :], tiles_f[:, :], ALU.subtract)
            V.tensor_tensor(run[:, :, :], run[:, :, :], sums[:, :, :], ALU.subtract)
            dve.drain()
            V.scalar_tensor_tensor(offset[:, :], tiles_f[:, :], float(TS), offset[:, :], ALU.mult, ALU.add)
            dve.drain()
            V.tensor_tensor(run[:, :, :], run[:, :, :], offset[:, :].unsqueeze(2).to_broadcast([P, NE, NCH]), ALU.add)
            dve.drain()
            V.tensor_tensor(slot[Q], run[Q, :, :].rearrange("p e c -> p c e"),
                            bank[7][Q, 0:NCH * NE].rearrange("p (c e) -> p c e", e=NE), ALU.add)
            V.tensor_tensor(passed[:, :, :], tile_no[:, :].unsqueeze(2).to_broadcast([P, NT + 1, NE]),
                            tile_end[:, :].unsqueeze(1).to_broadcast([P, NT + 1, NE]), ALU.is_ge)
            dve.drain()
            V.tensor_reduce(expert_f[:, :], passed[:, :, :], AX, ALU.add)
            dve.drain()
            V.tensor_scalar(expert_i[:, :], expert_f[:, :], float(NE - 1), None, ALU.min)
            for k, mine in enumerate(("first", "second")):
                V.tensor_tensor(a[Q], slot[Q], R[mine][Q], ALU.mult)
                dve.drain()
                V.tensor_reduce(pick[Q, :], a[Q], AX, ALU.add)
                dve.drain()
                V.tensor_copy(slot_i[k][Q, :], pick[Q, :])
                dve.drain()
            dve.drain().then_inc(routed, 1)

            dve.wait_ge(b2_in, 16)
            dve.sem_inc(y_copied, 2)
            for i in range(2):
                dve.sem_inc(y_stored[i], 1)
            with dve.Fori(0, NTP) as r:
                for i in range(2):
                    e = dve.value_load(expert_i[0:1, bass.ds(2 * r + i, 1)], min_val=0, max_val=NE - 1)
                    hold(dve, y_stored[i], 16 * r + 1)
                    hold(dve, y_ready, 2 * r + i + 1)
                    V.tensor_tensor(y[i][:, :, :], bank[6 + i][:, :].rearrange("p (h d) -> p h d", h=2),
                                    b2_b[:, bass.ds(e, 1), :].to_broadcast([P, 2, D]), ALU.add)
                    dve.drain().then_inc(y_copied, 1)

            for i in range(2):
                dve.sem_inc(out_stored[i], 1)
            with dve.Fori(0, NPAIR) as r:
                for i in range(2):
                    hold(dve, x2_in[i], 16 * r + 16)
                    hold(dve, y_gathered[i], (r + 1) * (32 * BC))
                    for k in range(2):
                        for c in range(BC):
                            V.scalar_tensor_tensor(comb[i][2][:, c, :], comb[i][k][:, c, :],
                                                   prob[k][Q, bass.ds((2 * r + i) * BC + c, 1)],
                                                   comb[i][2][:, c, :], ALU.mult, ALU.add)
                        dve.drain()
                    dve.drain().then_inc(combined, 1)

        @block.scalar
        def _(act):
            A = nc.scalar
            act.wait_ge(small_T, 1)
            A.copy(wgT[:, :, :].rearrange("p k e -> p (k e)"), bank[0][:, 0:DK * NE])
            A.copy(b1c[:, :], bank[1][:, 0:NE * HB])
            act.drain().then_inc(small_copied, 1)
            def std_out(s, b):
                hold(act, norm[s]["var_ready"], b + 1)
                A.activation(std[:, :], var[:, :], ACT.Sqrt).then_inc(norm[s]["std_ready"], 1)

            def turned_out(s, b, i, dest, between):
                q = norm[s]
                for c in range(BC + 1):
                    n = BC * i + c
                    if c < BC:
                        hold(act, q["xT_ready"], BC * b + c + 1)
                        A.copy(xT[n % 2][:, :, :].rearrange("p k c -> p (k c)"), bank[n % 2][:, 0:DK * CH]).then_inc(q["xT_copied"], 1)
                    if c:
                        hold(act, q["mm_ready"], BC * b + c)
                        dest((n - 1) % 2, BC * b + c - 1)
                    if c == 2 and between:
                        std_out(s, b + 1)

            def h_out(s, n):
                A.copy(feat[0:F, bass.ds(n * CH, CH)], bank[2 + s][0:F, 0:CH]).then_inc(norm[0]["mm_copied"], 1)

            def logit_out(s, n):
                A.copy(logit[:, bass.ds(n, 1), :].rearrange("p o e -> p (o e)"), bank[2 + s][0:CH, 0:NE]).then_inc(norm[1]["mm_copied"], 1)

            def first_block(b, i, between=True):
                turned_out(0, b, i, h_out, between)
                act.drain().then_inc(x_free[0][i], 1)

            def weights_out(e):
                for k, (stage, dram) in enumerate(((w1_out, w1t_d), (w2_out, w2t_d))):
                    hold(act, w_out[k], 16 * e + 1)
                    for n in range(4):
                        hold(act, w_T, 8 * e + 4 * k + n + 1)
                        A.copy(stage[:, n * 512:(n + 1) * 512], bank[4 + n % 2][:, :]).then_inc(w_evac, 1)
                    act.drain()
                    act.dma_start(dram[:, bass.ds(e, 1), :].rearrange("p o c -> p (o c)"), stage).then_inc(w_out[k], 16)

            act.sem_inc(w_evac, 2)
            for k in range(2):
                act.sem_inc(w_out[k], 1)
            std_out(0, 0)
            with act.Fori(0, NPAIR - 1) as r:
                for i in range(2):
                    first_block(2 * r + i, i)
                    weights_out(2 * r + i)
            first_block(2 * NPAIR - 2, 0)
            first_block(2 * NPAIR - 1, 1, between=False)

            act.wait_ge(deg_in, 16)
            A.activation(deg_few[:, :], deg_few[:, :], ACT.Sqrt).then_inc(sqrt_out, 1)

            def counts_out(l):
                L = layer[l]
                act.sem_inc(L["evac"], len(PIECES))
                for k in range(2):
                    act.wait_ge(w_out[k], 16 * NE + 1)
                with act.Fori(0, act_passes) as j:
                    with act.Fori(0, STEPS) as st:
                        for i in range(SA):
                            b = 0
                            for k, nb in enumerate(PIECES):
                                hold(act, L["counted"], ((j * STEPS + st) * SA + i) * len(PIECES) + k + 1)
                                A.copy(counts[:, b:b + nb, i, :], bank[2 + k][:, 0:nb * WA].rearrange("p (b w) -> p b w", w=WA)).then_inc(L["evac"], 1)
                                b += nb

            act.wait_ge(passes_ready, 1)
            act_passes = act.value_load(passes_i[0:1, 0:1], min_val=1, max_val=MOST)
            counts_out(0)
            counts_out(1)
            act.wait_ge(agg_done, 1)
            act.sem_inc(z_ready, 2)

            def feat_out(b, i):
                for c in range(BC):
                    hold(act, z_ready, BC * b + c + 1)
                    A.copy(fchunk[(BC * i + c) % 2], feat[:, bass.ds((BC * b + c) * CH, CH)]).then_inc(f_copied, 1)

            def second_block(b, i, between=True):
                if between:
                    feat_out(b + 1, 1 - i)
                turned_out(1, b, i, logit_out, between)
                act.drain().then_inc(xnb_turned, 1)

            feat_out(0, 0)
            std_out(1, 0)
            with act.Fori(0, NPAIR - 1) as r:
                for i in range(2):
                    second_block(2 * r + i, i)
            second_block(2 * NPAIR - 2, 0)
            second_block(2 * NPAIR - 1, 1, between=False)
            act.wait_ge(sel_ready, 1)
            A.activation(prob[1][0:CH, :], pick[0:CH, :], ACT.Exp).then_inc(exp_out, 1)

            act.wait_ge(tokT_ready, 1)
            A.copy(tokT[0][:, :, :].rearrange("p k t -> p (k t)"), bank[0][:, :]).then_inc(tokT_copied, 1)
            with act.Fori(0, NTP) as r:
                for i in range(2):
                    e = act.value_load(expert_i[0:1, bass.ds(2 * r + i, 1)], min_val=0, max_val=NE - 1)
                    for b in range(HB):
                        if b % 2 == 0:
                            hold(act, hid_ready, (2 * r + i) * (HB // 2) + b // 2 + 1)
                        A.activation(hid[:, b, :], bank[2 + b // 2][:, (b % 2) * TS:(b % 2 + 1) * TS], ACT.Relu,
                                     bias=b1c[:, bass.ds(e * HB + b, 1)]).then_inc(hid_copied, 1)
                    hold(act, tokT_ready, 2 * r + i + 2)
                    A.copy(tokT[1 - i][:, :, :].rearrange("p k t -> p (k t)"), bank[1 - i][:, :]).then_inc(tokT_copied, 1)

            with act.Fori(0, NPAIR) as r:
                for i in range(2):
                    hold(act, combined, 2 * r + i + 1)
                    act.dma_start(out_blk[bass.ds(2 * r + i, 1)].rearrange("o p c d -> (o p) c d"), comb[i][2]).then_inc(out_stored[i], 16)
            for i in range(2):
                act.wait_ge(out_stored[i], 16 * NPAIR + 1)

        @block.tensor
        def _(pe):
            T = nc.tensor
            pe.wait_ge(consts, 1)
            pe.wait_ge(weights_in, 112)
            for k in range(DK):
                T.transpose(bank[0][:, k * NE:(k + 1) * NE], wg_in[:, k * P:(k + 1) * P], ident[0:NE, 0:NE])
            T.transpose(bank[1][:, 0:NE * HB], b1_in[:, :], ident[0:NE * HB, 0:NE * HB])
            pe.drain().then_inc(small_T, 1)
            pe.wait_ge(small_copied, 1)
            def turn_block(s, b, i, source, product):
                q = norm[s]
                hold(pe, q["xn_ready"], b + 1)

                def turn(c):
                    for k in range(DK):
                        last = T.transpose(bank[(BC * i + c) % 2][:, k * CH:(k + 1) * CH], source[i][:, c, k * P:(k + 1) * P], ident[0:CH, 0:CH])
                    last.then_inc(q["xT_ready"], 1)

                turn(0)
                for c in range(BC):
                    if c + 1 < BC:
                        turn(c + 1)
                    hold(pe, q["xT_copied"], BC * b + c + 1)
                    product((BC * i + c) % 2).then_inc(q["mm_ready"], 1)

            def h_product(slot):
                for k in range(DK):
                    last = T.matmul(bank[2 + slot][0:F, 0:CH], gw1[:, k, :], xT[slot][:, k, :], start=k == 0, stop=k == DK - 1)
                return last

            def turn_weights(e):
                for k in range(2):
                    hold(pe, w_in[k], 16 * e + 16)
                    for n in range(4):
                        hold(pe, w_evac, 8 * e + 4 * k + n + 1)
                        for m in range(4):
                            if k == 0:
                                q, b = n // 2, 4 * (n % 2) + m
                                block_in = w1_in[:, b, q * P:(q + 1) * P]
                            else:
                                q, b = (4 * n + m) % DK, (4 * n + m) // DK
                                block_in = w2_in[:, q, b * P:(b + 1) * P]
                            last = T.transpose(bank[4 + n % 2][:, m * P:(m + 1) * P], block_in, ident[:, :])
                        last.then_inc(w_T, 1)
                    pe.drain().then_inc(w_used[k], 1)

            with pe.Fori(0, NPAIR - 1) as r:
                for i in range(2):
                    turn_block(0, 2 * r + i, i, xb, h_product)
                    turn_weights(2 * r + i)
            for i in range(2):
                turn_block(0, 2 * NPAIR - 2 + i, i, xb, h_product)
            pe.wait_ge(w_evac, 8 * NE + 2)
            pe.wait_ge(norm[0]["mm_copied"], NCH)

            pe.wait_ge(passes_ready, 1)
            passes = pe.value_load(passes_i[0:1, 0:1], min_val=1, max_val=MOST)

            def degrees(j, units, size, width, r0):
                with pe.Fori(0, units // 2) as g:
                    for i in range(2):
                        r = j * UNITS + r0 + g
                        hold(pe, deg_done["deg_hot"][i], r + 1)
                        hold(pe, deg_done["deg_acc"][i], r + 1)
                        for m in range(size):
                            for t in range(TE):
                                last = T.matmul(bank[2 * i + m // 4][0:F, (m % 4) * width:(m % 4 + 1) * width], ones_bf[:, :],
                                                hot_deg[i][:, 0:width, m * TE + t], start=t == 0, stop=t == TE - 1)
                        last.then_inc(deg_done["deg_mm"][i], 1)

            def table_turn(l):
                for b in range(NCB // TB):
                    pe.wait_ge(scaled, (NCB // TB) * l + b + 1)
                    pe.wait_ge(tabT_copied, (NCB // TB) * l + b + 1)
                    for c in range(TB):
                        last = T.transpose(bank[2 + b % 2][:, c * F:(c + 1) * F],
                                           feat[0:F, (TB * b + c) * P:(TB * b + c + 1) * P], ident[0:F, 0:F])
                    last.then_inc(tabT, 1)
                pe.wait_ge(tabT_copied, (NCB // TB) * (l + 1) + 2)

            def aggregate(l):
                L = layer[l]
                pe.sem_inc(L["used_a"], UR)
                for i in range(2):
                    pe.sem_inc(L["done_b"][i], 1)
                with pe.Fori(0, passes) as j:
                    with pe.Fori(0, STEPS // 2) as st:
                        turn = j * (STEPS // 2) + st

                        def count_a(i):
                            for t in range(TE):
                                hold(pe, L["hot_a"], j * TILES_A + st * (2 * SA * TE) + i * TE + t + 1)
                                b = 0
                                for k, nb in enumerate(PIECES):
                                    if t == 0:
                                        hold(pe, L["evac"], turn * (2 * SA * len(PIECES)) + i * len(PIECES) + k + 1)
                                    mm = T.matmul(bank[2 + k][:, 0:nb * WA], hot_lo[i % 2][:, t, :], hot_key[t % UR][:, b * WA:(b + nb) * WA],
                                                  start=t == 0, stop=t == TE - 1)
                                    b += nb
                                    if t == TE - 1:
                                        mm.then_inc(L["counted"], 1)
                                if t < TE - 1:
                                    mm.then_inc(L["used_a"], 1)
                            pe.drain().then_inc(L["used_a"], 1)

                        def sum_b(i):
                            s = i % 2
                            hold(pe, L["hot_b"], turn * (2 * SB) + i + 1)
                            hold(pe, L["acc_b"], turn * (2 * SB) + i + 1)
                            hold(pe, L["gathered"][s], (turn * SB + i // 2 + 1) * (16 * TE))
                            for t in range(TE):
                                for k in range(3):
                                    last = T.matmul(bank[s][0:F, 0:WB], rows[s][:, t, k, :], hot_b[s][:, t, :],
                                                    start=t == 0 and k == 0, stop=t == TE - 1 and k == 2)
                            last.then_inc(L["done_b"][s], 1)

                        def product(half):
                            hold(pe, L["evac"], (turn * 2 + half + 1) * (SA * len(PIECES)) + len(PIECES))
                            hold(pe, L["summed"], turn * 2 + half + 1)
                            for b in range(NCB):
                                for k in range(3):
                                    last = T.matmul(bank[6][0:F, 0:SA * WA], parts[:, b, k, :],
                                                    counts[:, b, :, :].rearrange("p i w -> p (i w)"),
                                                    start=b == 0 and k == 0, stop=b == NCB - 1 and k == 2)
                            last.then_inc(L["product"], 1)

                        for half in range(2):
                            for i in range(SA):
                                count_a(half * SA + i)
                                sum_b(half * SB + i)
                            product(half)
                            sum_b(half * SB + SA)
                    hold(pe, L["hot_a"], (j + 1) * TILES_A)
                    pe.sem_inc(L["used_a"], UR)

            for i in range(2):
                pe.sem_inc(deg_done["deg_mm"][i], 1)
            with pe.Fori(0, passes) as j:
                degrees(j, NA // UA, UA, WA, 0)
                degrees(j, NB // UB, UB, WB, NA // UA // 2)
            for l in range(2):
                table_turn(l)
                aggregate(l)

            pe.wait_ge(agg_done, 1)
            pe.sem_inc(z_used, 2)

            def z_block(b, i):
                for c in range(BC):
                    n = (BC * i + c) % 2
                    hold(pe, z_used, BC * b + c + 1)
                    hold(pe, f_copied, BC * b + c + 1)
                    T.matmul(bank[4 + n][0:CH, 0:D], fchunk[n], gw2[:, :], start=True, stop=True).then_inc(z_ready, 1)

            def gate_product(slot):
                for k in range(DK):
                    last = T.matmul(bank[2 + slot][0:CH, 0:NE], xT[slot][:, k, :], wgT[:, k, :], start=k == 0, stop=k == DK - 1)
                return last

            def second_block(b, i, ahead=True):
                if ahead:
                    z_block(b + 1, 1 - i)
                turn_block(1, b, i, xnb, gate_product)

            z_block(0, 0)
            with pe.Fori(0, NPAIR - 1) as r:
                for i in range(2):
                    second_block(2 * r + i, i)
            second_block(2 * NPAIR - 2, 0)
            second_block(2 * NPAIR - 1, 1, ahead=False)

            pe.wait_ge(sel_ready, 1)
            sel = R["sel"][0:CH].rearrange("p c e -> p (c e)")
            T.matmul(bank[6][:, 0:NCH * NE], ones_s[0:CH, 0:P], sel, start=True, stop=True)
            T.matmul(bank[7][0:CH, 0:NCH * NE], below[0:CH, 0:CH], sel, start=True, stop=True).then_inc(prefix_ready, 1)

            def turn_tokens(i):
                for h in range(2):
                    for k in range(DK):
                        last = T.transpose(bank[i][:, k * TS + h * P:k * TS + (h + 1) * P], tok[i][:, h, k * P:(k + 1) * P], ident[:, :])
                last.then_inc(tokT_ready, 1)

            pe.wait_ge(routed, 1)
            pe.wait_ge(wt_loaded, 16)
            pe.wait_ge(tok_in[0], 16)
            turn_tokens(0)
            with pe.Fori(0, NTP) as r:
                for i in range(2):
                    e = pe.value_load(expert_i[0:1, bass.ds(2 * r + i, 1)], min_val=0, max_val=NE - 1)
                    hold(pe, tokT_copied, 2 * r + i + 1)
                    hold(pe, w1_loaded[i], 16 * r + 16)
                    for b in range(HB):
                        for k in range(DK):
                            last = T.matmul(bank[2 + b // 2][:, (b % 2) * TS:(b % 2 + 1) * TS],
                                            w1t[i][:, k * H + b * P:k * H + (b + 1) * P], tokT[i][:, k, :],
                                            start=k == 0, stop=k == DK - 1)
                        if b % 2:
                            last.then_inc(hid_ready, 1)
                    hold(pe, tok_in[1 - i], 16 * r + 16 * (1 + i))
                    turn_tokens(1 - i)
                    hold(pe, y_copied, 2 * r + i + 1)
                    for h in range(2):
                        for b in range(HB):
                            if h == 0:
                                hold(pe, hid_copied, (2 * r + i) * HB + b + 1)
                            last = T.matmul(bank[6 + i][:, h * D:(h + 1) * D], hid[:, b, h * P:(h + 1) * P],
                                            w2t[:, bass.ds(e * (HB * D) + b * D, D)], start=b == 0, stop=b == HB - 1)
                    last.then_inc(y_ready, 1)


_INS = ['x', 'src', 'dst', 'L0_gnn_W1', 'L0_gnn_b1', 'L0_gnn_W2', 'L0_gnn_b2', 'L0_ffn_Wg', 'L0_ffn_bg',
        'L0_ffn_W1', 'L0_ffn_b1', 'L0_ffn_W2', 'L0_ffn_b2']


def kernel(**inputs):
    import numpy as np
    import concourse.bacc as bacc
    from concourse import mybir as mb
    from concourse.bass_utils import run_bass_kernel_spmd as run

    nc = bacc.Bacc("TRN2", target_bir_lowering=False, num_devices=1)
    arrays, args = {}, []
    for name in _INS:
        a = np.ascontiguousarray(inputs[name])
        arrays[f"in_{name}"] = a
        args.append(nc.dram_tensor(f"in_{name}", a.shape, mb.dt.from_np(a.dtype), kind="ExternalInput").ap())
    o = nc.dram_tensor("out_x", (N, D), mb.dt.float32, kind="ExternalOutput").ap()
    gnn_moe(nc, *args, o)
    r = run(nc, [arrays], core_ids=[0])
    return r.results[0]["out_x"]
```

```python
import concourse.bass as bass
from concourse import mybir
from contextlib import ExitStack

F32 = mybir.dt.float32
BF16 = mybir.dt.bfloat16
F16 = mybir.dt.float16
I32 = mybir.dt.int32
ALU = mybir.AluOpType
ACT = mybir.ActivationFunctionType
AX = mybir.AxisListType.X

P = 128
N, D = 6250, 256
F = 64
EDGES = 200000
NE, H = 8, 1024
DK, HB = D // P, H // P
EPS = 1e-5

CH = 125
NCH = N // CH
BC = 5
NPAIR = NCH // BC // 2

TE = 8
GE = TE * P
NCB = -(-N // P)
NCAP = NCB * P

STEPS, SA, SB = 22, 4, 5
NA, NB = STEPS * SA, STEPS * SB
NG = NA + NB
WA, WB = 32, 72
AW = NCAP + WB
KEYS = NCB * WA
PIECES = (13, 12, 12, 12)
UR = 4
TILES_A = NA * TE + UR
LO = 64
HI = NCAP // LO
UT = 4 * TE
UNITS = -(-EDGES // (UT * P))
FULL_G = EDGES // GE
TAIL_P = (EDGES - FULL_G * GE) // TE
MOST = NCAP // WA + 1
assert sum(PIECES) == NCB and max(PIECES) * WA <= 512 and KEYS <= 2048
assert NG * GE >= EDGES and GE <= 2048
TB = 7
assert NCB % TB == 0

TS = 256
NT = (2 * N + NE * (TS - 1)) // TS
NTP = NT // 2
LEAST = 2 * -(-N // TS)
SHIFT = TS.bit_length() - 1
ZR = 8
ZD = -(-(NT + 1) * TS // (NPAIR * P * ZR))
SLOTS = ZD * NPAIR * P * ZR
BIG = 3.0e38
assert BC * (2 * NPAIR - 1) <= UNITS <= NCH and STEPS % 2 == 0 and NCAP % LO == 0
assert NT % 2 == 0 and N == CH * NCH and NE == 2 * (NPAIR - 1) and NCH == 2 * BC * NPAIR


def gnn_moe(nc, x, src, dst, gW1, gb1, gW2, gb2, Wg, bg, eW1, eb1, eW2, eb2, out):
    table = [nc.dram_tensor(f"table{l}", (NCAP, 3 * F), BF16).ap() for l in range(2)]
    dinv_d = nc.dram_tensor("dinv_d", (NCAP,), F32).ap()
    w1t_d = nc.dram_tensor("w1t_d", (P, NE, DK * H), F32).ap()
    w2t_d = nc.dram_tensor("w2t_d", (P, NE, HB * D), F32).ap()
    x2_d = nc.dram_tensor("x2_d", (N, D), F32).ap()
    slots_x = nc.dram_tensor("slots_x", (SLOTS, D), F32).ap()
    slots_y = nc.dram_tensor("slots_y", (NT * TS, D), F32).ap()

    ctx = ExitStack()
    with ctx:
        def sb(name, shape, dt=F32):
            return ctx.enter_context(nc.sbuf_tensor(name, shape, dt))

        def sem(name):
            return ctx.enter_context(nc.semaphore(name))

        arena = sb("arena", [P, NE * (DK * H + HB * D)])
        taken = [0]

        def carve(parts, cols):
            a = arena[0:parts, taken[0]:taken[0] + cols]
            taken[0] += cols
            return a

        feat = carve(F + 1, AW)
        dinv_space = carve(P, AW)
        dinv = dinv_space[0:F, :]
        hot_deg = [dinv_space[:, i * ((LO + HI) * UT // 2):(i + 1) * ((LO + HI) * UT // 2)].bitcast(BF16).rearrange("p (v t) -> p v t", v=LO + HI) for i in range(2)]
        xb = [carve(CH, BC * D).rearrange("p (c d) -> p c d", c=BC) for _ in range(2)]
        rows_space = [carve(P, TE * 3 * F // 2) for _ in range(2)]
        rows = [a.bitcast(BF16).rearrange("p (t k f) -> p t k f", t=TE, k=3) for a in rows_space]
        fblock = [a[0:F + 1, 0:BC * CH] for a in rows_space]
        hot_b = [carve(P, TE * WB // 2).bitcast(BF16).rearrange("p (t w) -> p t w", t=TE) for _ in range(2)]
        dst_i = carve(P, NG * TE).bitcast(I32).rearrange("p (g t) -> p g t", t=TE)
        src_i = carve(P, NG * TE).bitcast(I32).rearrange("p (g t) -> p g t", t=TE)
        dst_f = carve(P, NG * TE).rearrange("p (g t) -> p g t", t=TE)
        key = carve(P, NG * TE).rearrange("p (g t) -> p g t", t=TE)
        src_lo = carve(P, (NA + 1) * TE).rearrange("p (g t) -> p g t", t=TE)
        src_hi = carve(P, NA * TE).rearrange("p (g t) -> p g t", t=TE)
        span_in = carve(P, 2 * NG)
        span = carve(P, 2 * NG)
        base0 = carve(P, NG)
        base_f = carve(P, NG)
        base_i = carve(P, NG).bitcast(I32)
        in_win = carve(P, NA * TE).rearrange("p (g t) -> p g t", t=TE)
        zeros = carve(P, ZR * D)
        xnb = [carve(CH, BC * D).rearrange("p (c d) -> p c d", c=BC) for _ in range(2)]
        assert taken[0] <= NE * (DK * H + HB * D)
        w1t = [arena[:, i * DK * H:(i + 1) * DK * H] for i in range(2)]
        w2t = arena[:, NE * DK * H:NE * (DK * H + HB * D)]

        ones_bf = sb("ones_bf", [P, F], BF16)
        ident = sb("ident", [P, P])
        deg_few = sb("deg_few", [HI, LO])
        iota_1 = sb("iota_1", [P, KEYS], F16)
        rest = [sb(f"rest{i}", [P, TB * F]).rearrange("p (b f) -> p b f", f=F) for i in range(2)]
        lo_s = [sb(f"lo_s{i}", [P, TE], F16) for i in range(2)]
        key_s = [sb(f"key_s{i}", [P, TE]) for i in range(2)]
        keyb_s = [sb(f"keyb_s{i}", [P, TE], F16) for i in range(2)]
        widest = sb("widest", [P, 3])
        reached = sb("reached", [P, 2, MOST])
        passes_i = sb("passes_i", [P, 1], I32)
        idx = [sb(f"idx{i}", [P, SB, TE], I32) for i in range(2)]
        gw1 = sb("gw1", [P, DK, F])
        gw2 = sb("gw2", [F + 1, D])
        gb1c = sb("gb1c", [F, 1])
        xT = [sb(f"xT{i}", [P, DK, CH]) for i in range(2)]
        stats = sb("stats", [CH, BC, 6])
        mv = sb("mv", [CH, BC, 2])
        var = sb("var", [CH, BC])
        std = sb("std", [CH, BC])
        rstd = sb("rstd", [CH, BC])
        room = sb("room", [P, NCH * D])
        w1_in = room[:, 0:HB * D].rearrange("p (b d) -> p b d", b=HB)
        w2_in = room[:, 2048:4096].rearrange("p (b h) -> p b h", b=DK)
        w1_out = room[:, 4096:6144]
        w2_out = room[:, 6144:8192]
        counts = room[:, 0:KEYS * SA // 2].bitcast(F16).rearrange("p (b i w) -> p b i w", b=NCB, i=SA)
        at = KEYS * SA // 2
        hot_key = [room[:, at + i * (KEYS // 2):at + (i + 1) * (KEYS // 2)].bitcast(BF16) for i in range(UR)]
        at += UR * (KEYS // 2)
        hot_lo = [room[:, at + i * (TE * P // 2):at + (i + 1) * (TE * P // 2)].bitcast(BF16).rearrange("p (t n) -> p t n", t=TE) for i in range(2)]
        at += TE * P
        parts = room[:, at:at + NCB * 3 * F // 2].bitcast(BF16).rearrange("p (b k f) -> p b k f", b=NCB, k=3)
        assert at + NCB * 3 * F // 2 <= NCH * D
        iota_t = room[:, 8192:8192 + HI * UT // 2].bitcast(F16).rearrange("p (v t) -> p v t", v=HI)
        low_16, high_16 = (room[:, 8192 + (HI * UT + k * NG * TE) // 2:8192 + (HI * UT + (k + 1) * NG * TE) // 2].bitcast(F16) for k in range(2))
        xn = room[0:CH, :].rearrange("p (c d) -> p c d", d=D)
        tok = [room[:, i * 512:(i + 1) * 512].rearrange("p (h d) -> p h d", h=2) for i in range(2)]
        tokT = [room[:, 1024 + i * 512:1024 + (i + 1) * 512].rearrange("p (k t) -> p k t", k=DK) for i in range(2)]
        hid = room[:, 2048:2048 + HB * TS].rearrange("p (b t) -> p b t", b=HB)
        b2_b = room[:, 5120:5120 + NE * D].rearrange("p (e d) -> p e d", e=NE)
        y = [room[:, 4096 + i * 512:4096 + (i + 1) * 512].rearrange("p (h d) -> p h d", h=2) for i in range(2)]
        wg_in = sb("wg_in", [NE, D])
        wgT = sb("wgT", [P, DK, NE])
        bg_b = sb("bg_b", [CH, NE])
        logit = sb("logit", [CH, NCH, NE])

        def scratch_of(k, cols):
            return arena[:, AW + k:AW + k + cols]

        R = {n: scratch_of(i * NCH * NE, NCH * NE).rearrange("p (c e) -> p c e", e=NE)
             for i, n in enumerate(("a", "first", "second", "sel", "slot"))}
        sums, run = (scratch_of(k * NCH * NE, NCH * NE).rearrange("p (e c) -> p e c", e=NE) for k in (5, 6))
        passed = scratch_of(7 * NCH * NE, (NT + 1) * NE).rearrange("p (t e) -> p t e", e=NE)
        ones_s = sb("ones_s", [P, NE * NCH])
        rev = sb("rev", [P, NE])
        best = [sb(f"best{i}", [P, NCH]) for i in range(2)]
        pick = sb("pick", [P, NCH])
        prob = [sb(f"prob{i}", [P, NCH]) for i in range(2)]
        slot_i = [sb(f"slot_i{i}", [P, NCH], I32) for i in range(2)]
        below = sb("below", [P, P])
        count = sb("count", [P, NE])
        tiles_i = sb("tiles_i", [P, NE], I32)
        tiles_f = sb("tiles_f", [P, NE])
        tile_end = sb("tile_end", [P, NE])
        offset = sb("offset", [P, NE])
        tile_no = sb("tile_no", [P, NT + 1])
        expert_f = sb("expert_f", [P, NT + 1])
        expert_i = sb("expert_i", [P, NT + 1], I32)
        pairs_i = sb("pairs_i", [P, 1], I32)

        b1_in = sb("b1_in", [NE * HB, P])
        b1c = sb("b1c", [P, NE * HB])

        bank = [ctx.enter_context(nc.psum_tensor(f"bank{i}", [P, 512], F32)) for i in range(8)]

        consts = sem("consts")
        weights_in = sem("weights_in")
        dst_in, src_in = sem("dst_in"), sem("src_in")
        pads_set = sem("pads_set")
        zero_set = sem("zero_set")
        slots_zeroed = sem("slots_zeroed")
        tick = sem("tick")
        small_T = sem("small_T")
        small_copied = sem("small_copied")
        w_in = [sem(f"w_in{k}") for k in range(2)]
        w_T = sem("w_T")
        w_evac = sem("w_evac")
        w_used = [sem(f"w_used{k}") for k in range(2)]
        w_out = [sem(f"w_out{k}") for k in range(2)]
        span_ready = sem("span_ready")
        span_reduced = sem("span_reduced")
        passes_ready = sem("passes_ready")
        deg_hot, deg_used = sem("deg_hot"), sem("deg_used")
        deg_ready, sqrt_out, dinv_ready = sem("deg_ready"), sem("sqrt_out"), sem("dinv_ready")
        dinv_stored, dinv_in = sem("dinv_stored"), sem("dinv_in")
        scaled = sem("scaled")
        tabT, tabT_read, split = sem("tabT"), sem("tabT_read"), sem("split")
        high_ready, left_ready, mid_ready = sem("high_ready"), sem("left_ready"), sem("mid_ready")
        tab_stored = [sem(f"tab_stored{l}") for l in range(2)]
        agg_done = sem("agg_done")
        norm = [{n: sem(f"{n}_{s}") for n in
                 ("var_ready", "std_ready", "xn_ready", "xT_ready", "xT_copied", "mm_ready", "mm_copied", "x2_ready")}
                for s in ("first", "second")]
        x_in = [[sem(f"x_in{s}{i}") for i in range(2)] for s in range(2)]
        x_free = [[sem(f"x_free{s}{i}") for i in range(2)] for s in range(2)]
        z_ready, z_used = sem("z_ready"), sem("z_used")
        x2_stored = [sem(f"x2_stored{i}") for i in range(2)]
        layer = [{n: sem(f"{n}_{l}") for n in
                  ("hot_a", "used_a", "counted", "evac", "product", "summed", "hot_b", "acc_b", "idx_ready", "gathered_reset")}
                 | {n: [sem(f"{n}_{l}{i}") for i in range(2)] for n in ("gathered", "done_b")}
                 for l in range(2)]
        logits_done = sem("logits_done")
        exp_out = sem("exp_out")
        sel_ready, prefix_ready = sem("sel_ready"), sem("prefix_ready")
        routed = sem("routed")
        scattered = sem("scattered")
        wt_loaded = sem("wt_loaded")
        b2_in = sem("b2_in")
        w1_loaded = [sem(f"w1_loaded{i}") for i in range(2)]
        xnb_turned, xnb_kept = sem("xnb_turned"), sem("xnb_kept")
        f_copied = sem("f_copied")
        tok_in = [sem(f"tok_in{i}") for i in range(2)]
        tokT_ready, tokT_copied = sem("tokT_ready"), sem("tokT_copied")
        hid_ready, hid_copied = sem("hid_ready"), sem("hid_copied")
        y_ready, y_copied = sem("y_ready"), sem("y_copied")
        y_stored = [sem(f"y_stored{i}") for i in range(2)]
        cidx_ready = [sem(f"cidx_ready{i}") for i in range(2)]
        y_gathered = [sem(f"y_gathered{i}") for i in range(2)]
        x2_in = [sem(f"x2_in{i}") for i in range(2)]
        combined = sem("combined")
        out_stored = [sem(f"out_stored{i}") for i in range(2)]

        x_blk = x.rearrange("(b c p) d -> b p c d", c=BC, p=CH)
        x2_blk = x2_d.rearrange("(b c p) d -> b p c d", c=BC, p=CH)
        out_blk = out.rearrange("(b c p) d -> b p c d", c=BC, p=CH)
        zero_rows = slots_x.rearrange("(i z p r) d -> i z p r d", i=NPAIR, z=ZD, p=P)
        sx_t = slots_x.rearrange("(t h p) d -> t p h d", h=2, p=P)
        sy_t = slots_y.rearrange("(t h p) d -> t p h d", h=2, p=P)
        comb = [[arena[0:CH, (3 * i + k) * BC * D:(3 * i + k + 1) * BC * D].rearrange("p (c d) -> p c d", c=BC)
                 for k in range(3)] for i in range(2)]
        cidx = [[sb(f"cidx{i}{k}", [P, BC], I32) for k in range(2)] for i in range(2)]

        def turned(m):
            return bank[2 + m % 2][:, 0:TB * F].rearrange("p (b f) -> p b f", f=F)

        def hold(eng, s, value):
            eng.wait_ge(s, value)
            eng.sem_inc(tick, 1)

        block = ctx.enter_context(nc.Block())

        @block.sync
        def _(sp):
            def load_x(s, r, i):
                hold(sp, x_free[s][i], r + 1)
                sp.dma_start(xb[i], x_blk[bass.ds(2 * r + i, 1)].rearrange("o p c d -> (o p) c d")).then_inc(x_in[s][i], 16)

            sp.wait_ge(pads_set, 1)
            sp.dma_start(dst_i[:, 0:FULL_G, :], dst[0:FULL_G * GE].rearrange("(g p t) -> p g t", p=P, t=TE)).then_inc(dst_in, 16)
            sp.dma_start(dst_i[0:TAIL_P, FULL_G, :], dst[FULL_G * GE:EDGES].rearrange("(p t) -> p t", t=TE)).then_inc(dst_in, 16)
            sp.dma_start(wg_in[:, :], Wg).then_inc(weights_in, 16)
            sp.dma_start(b1_in[:, :], eb1.rearrange("e (b p) -> (e b) p", p=P)).then_inc(weights_in, 16)
            sp.dma_start(gw1[:, :, :], gW1.rearrange("(k p) f -> p k f", p=P)).then_inc(weights_in, 16)
            sp.dma_start(gw2[0:F, :], gW2).then_inc(weights_in, 16)
            sp.dma_start(gw2[F:F + 1, :], gb2.rearrange("(o d) -> o d", o=1)).then_inc(weights_in, 16)
            sp.dma_start(gb1c[:, :], gb1.rearrange("(f o) -> f o", o=1)).then_inc(weights_in, 16)
            sp.dma_start(bg_b[:, :], bg.rearrange("(o e) -> o e", o=1).to_broadcast([CH, NE])).then_inc(weights_in, 16)
            sp.wait_ge(zero_set, 1)
            with sp.Fori(0, NPAIR) as r:
                for i in range(2):
                    load_x(0, r, i)
                sp.dma_start(zero_rows[bass.ds(r, 1)].rearrange("o z p r d -> (o p) z (r d)"),
                             zeros.unsqueeze(1).to_broadcast([P, ZD, ZR * D])).then_inc(slots_zeroed, 16)
            sp.dma_start(src_i[:, 0:FULL_G, :], src[0:FULL_G * GE].rearrange("(g p t) -> p g t", p=P, t=TE)).then_inc(src_in, 16)
            sp.dma_start(src_i[0:TAIL_P, FULL_G, :], src[FULL_G * GE:EDGES].rearrange("(p t) -> p t", t=TE)).then_inc(src_in, 16)
            sp.dma_start(slots_y[LEAST * TS:NT * TS, :].rearrange("(z p r) d -> p z (r d)", p=P, r=TS // P),
                         zeros[:, 0:TS // P * D].unsqueeze(1).to_broadcast([P, NT - LEAST, TS // P * D])).then_inc(slots_zeroed, 16)
            sp.wait_ge(dinv_ready, 1)
            sp.dma_start(dinv_d.rearrange("(h l) -> h l", l=LO), deg_few[:, :]).then_inc(dinv_stored, 16)
            sp.wait_ge(dinv_stored, 16)
            sp.dma_start(dinv[:, 0:NCAP], dinv_d.rearrange("(o n) -> o n", o=1).to_broadcast([F, NCAP])).then_inc(dinv_in, 16)
            for l in range(2):
                for m in range(NCB // TB):
                    sp.wait_ge(split, (NCB // TB) * l + m + 1)
                    b = slice(m * TB, (m + 1) * TB)
                    sp.dma_start(table[l].rearrange("(c p) f -> p c f", p=P)[:, b],
                                 parts[:, b].rearrange("p b k f -> p b (k f)")).then_inc(tab_stored[l], 16)
            for i in range(2):
                sp.sem_inc(x2_stored[i], 1)
            with sp.Fori(0, NPAIR) as r:
                for i in range(2):
                    hold(sp, x2_stored[i], 16 * r + 1)
                    load_x(1, r, i)
                for i in range(2):
                    hold(sp, norm[1]["x2_ready"], 2 * r + i + 1)
                    sp.dma_start(x2_blk[bass.ds(2 * r + i, 1)].rearrange("o p c d -> (o p) c d"), xb[i]).then_inc(x2_stored[i], 16)
            sp.wait_ge(logits_done, 1)
            sp.wait_ge(xnb_turned, 2 * NPAIR + 2)
            sp.wait_ge(xnb_kept, 2 * NPAIR + 2)
            for i in range(2):
                sp.wait_ge(x2_stored[i], 16 * NPAIR + 1)
            for k in range(2):
                sp.wait_ge(w_out[k], 16 * NE + 1)
            sp.wait_ge(slots_zeroed, 16 * NPAIR + 16)
            sp.dma_start(w2t, w2t_d.rearrange("p e c -> p (e c)")).then_inc(wt_loaded, 16)

            sp.wait_ge(routed, 1)

            def load_weights(t, i):
                e = sp.value_load(expert_i[0:1, bass.ds(t, 1)], min_val=0, max_val=NE - 1)
                sp.dma_start(w1t[i], w1t_d[:, bass.ds(e, 1), :].rearrange("p o c -> p (o c)")).then_inc(w1_loaded[i], 16)

            def load_tokens(t, i):
                sp.dma_start(tok[i][:, :, :], sx_t[bass.ds(t, 1)].rearrange("o p h d -> (o p) h d")).then_inc(tok_in[i], 16)

            sp.wait_ge(scattered, 16 * 2 * NCH)
            load_tokens(0, 0)
            load_weights(0, 0)
            sp.dma_start(b2_b, eb2.rearrange("(o e) d -> o e d", o=1).to_broadcast([P, NE, D])).then_inc(b2_in, 16)
            sp_pairs = sp.value_load(pairs_i[0:1, 0:1], min_val=1, max_val=NTP)
            with sp.Fori(0, sp_pairs) as r:
                for i in range(2):
                    hold(sp, tokT_ready, 2 * r + i + 1)
                    load_tokens(2 * r + i + 1, 1 - i)
                    load_weights(2 * r + i + 1, 1 - i)
                    hold(sp, y_copied, 2 * r + i + 3)
                    sp.dma_start(sy_t[bass.ds(2 * r + i, 1)].rearrange("o p h d -> (o p) h d"), y[i][:, :, :]).then_inc(y_stored[i], 16)
            for i in range(2):
                hold(sp, y_stored[i], 16 * sp_pairs + 1)
            with sp.Fori(0, NPAIR) as r:
                for i in range(2):
                    hold(sp, out_stored[i], 16 * r + 1)
                    sp.dma_start(comb[i][2], x2_blk[bass.ds(2 * r + i, 1)].rearrange("o p c d -> (o p) c d")).then_inc(x2_in[i], 16)

        @block.gpsimd
        def _(pool):
            nc.gpsimd.memset(dst_i[:, FULL_G:NG, :], N)
            nc.gpsimd.memset(src_i[:, FULL_G:NG, :], 0)
            pool.drain().then_inc(pads_set, 1)
            nc.gpsimd.memset(ident[:, :], 0.0)
            nc.gpsimd.memset(below[:, :], 1.0)
            nc.gpsimd.memset(ones_bf[:, :], 1.0)
            nc.gpsimd.memset(ones_s[:, :], 1.0)
            nc.gpsimd.iota(iota_1[:, :], [[1, KEYS]], base=1, channel_multiplier=0, allow_small_or_imprecise_dtypes=True)
            nc.gpsimd.iota(iota_t, [[1, HI], [0, UT]], base=0, channel_multiplier=0, allow_small_or_imprecise_dtypes=True)
            nc.gpsimd.iota(rev[:, :], [[-1, NE]], base=NE, channel_multiplier=0, allow_small_or_imprecise_dtypes=True)
            nc.gpsimd.iota(tile_no[:, :], [[1, NT + 1]], base=0, channel_multiplier=0, allow_small_or_imprecise_dtypes=True)
            pool.drain()
            nc.gpsimd.affine_select(out=ident[:, :], in_=ident[:, :], compare_op=ALU.not_equal, fill=1.0, base=0,
                                    pattern=[[-1, P]], channel_multiplier=1)
            nc.gpsimd.affine_select(out=below[:, :], in_=below[:, :], compare_op=ALU.is_gt, fill=0.0, base=0,
                                    pattern=[[1, P]], channel_multiplier=-1)
            pool.drain().then_inc(consts, 1)
            nc.gpsimd.memset(zeros, 0.0).then_inc(zero_set, 1)
            def load_expert(e, k):
                w, stage = ((eW1, w1_in), (eW2, w2_in))[k]
                pool.dma_start(stage, w[bass.ds(e, 1)].rearrange("o (b p) c -> p (o b) c", p=P)).then_inc(w_in[k], 16)

            for k in range(2):
                load_expert(0, k)
            with pool.Fori(1, NE) as e:
                for k in range(2):
                    hold(pool, w_used[k], e)
                    load_expert(e, k)
            pool.wait_ge(span_ready, 1)
            nc.gpsimd.partition_all_reduce(span[:, :], span_in[:, :], P, bass.bass_isa.ReduceOp.max).then_inc(span_reduced, 1)
            pool.wait_ge(passes_ready, 1)
            pool.wait_ge(src_in, 32)
            passes = pool.value_load(passes_i[0:1, 0:1], min_val=1, max_val=MOST)
            for l in range(2):
                L = layer[l]
                pool.wait_ge(tab_stored[l], 16 * (NCB // TB))
                pool.sem_inc(L["gathered_reset"], 1)
                with pool.Fori(0, passes) as j:
                    with pool.Fori(0, STEPS // 2) as st:
                        turn = j * (STEPS // 2) + st
                        for half in range(2):
                            nc.gpsimd.tensor_copy(idx[half][:, :, :], src_i[:, bass.ds(NA + (2 * st + half) * SB, SB), :]).then_inc(L["idx_ready"], 1)
                            hold(pool, L["idx_ready"], 2 * turn + half + 1)
                            for i in range(SB):
                                n = half * SB + i
                                hold(pool, L["done_b"][n % 2], turn * SB + n // 2 + 1)
                                for t in range(TE):
                                    pool.indirect_dma_start(rows[n % 2][:, t, :, :].rearrange("p k f -> p (k f)"), None, table[l],
                                                            bass.IndirectOffsetOnAxis(ap=idx[half][:, i, t:t + 1], axis=0)).then_inc(L["gathered"][n % 2], 16)
                    for s in range(2):
                        hold(pool, L["done_b"][s], (j + 1) * (NB // 2) + 1)
                    pool.inc_swdge_sem(L["gathered"], [NB // 2 * TE * 16] * 2, mode="sub")
                    pool.sem_inc(L["gathered_reset"], 1)
            pool.wait_ge(agg_done, 1)
            with pool.Fori(0, NPAIR) as r:
                for i in range(2):
                    hold(pool, norm[1]["xn_ready"], 2 * r + i + 1)
                    nc.gpsimd.tensor_copy(xn[:, bass.ds((2 * r + i) * BC, BC), :], xnb[i]).then_inc(xnb_kept, 1)
            pool.wait_ge(routed, 1)
            pool.wait_ge(xnb_kept, 2 * NPAIR + 2)
            pool.wait_ge(slots_zeroed, 16 * NPAIR + 16)
            for c in range(NCH):
                for k in range(2):
                    pool.indirect_dma_start(slots_x, bass.IndirectOffsetOnAxis(ap=slot_i[k][0:CH, c:c + 1], axis=0),
                                            xn[:, c, :], None).then_inc(scattered, 16)
            pool_pairs = pool.value_load(pairs_i[0:1, 0:1], min_val=1, max_val=NTP)
            for i in range(2):
                hold(pool, y_stored[i], 16 * pool_pairs + 1)
            with pool.Fori(0, NPAIR) as r:
                for i in range(2):
                    hold(pool, out_stored[i], 16 * r + 1)
                    for k in range(2):
                        nc.gpsimd.tensor_copy(cidx[i][k][0:CH, :], slot_i[k][0:CH, bass.ds((2 * r + i) * BC, BC)]).then_inc(cidx_ready[i], 1)
                    hold(pool, cidx_ready[i], 2 * r + 2)
                    for c in range(BC):
                        for k in range(2):
                            pool.indirect_dma_start(comb[i][k][:, c, :], None, slots_y,
                                                    bass.IndirectOffsetOnAxis(ap=cidx[i][k][0:CH, c:c + 1], axis=0)).then_inc(y_gathered[i], 16)

        @block.vector
        def _(dve):
            V = nc.vector

            def layer_norm(s, i, r, dest):
                q = norm[s]
                for c in range(BC):
                    V.bn_stats(stats[:, c, :], xb[i][:, c, :])
                dve.drain()
                for c in range(BC):
                    V.bn_aggr(mv[:, c, :], stats[:, c, :])
                dve.drain()
                V.tensor_scalar(var[:, :], mv[:, :, 1], EPS, None, ALU.add).then_inc(q["var_ready"], 1)
                hold(dve, q["std_ready"], 2 * r + i + 1)
                V.reciprocal(rstd[:, :], std[:, :])
                dve.drain()
                for c in range(BC):
                    V.tensor_scalar(dest(c), xb[i][:, c, :], mv[:, c, 0:1], rstd[:, c:c + 1], ALU.subtract, ALU.mult)
                dve.drain().then_inc(q["xn_ready"], 1)

            dve.wait_ge(dst_in, 32)
            destinations = dst_i.rearrange("p g t -> p (g t)")
            scratch = key.bitcast(I32).rearrange("p g t -> p (g t)")
            for part, op, value in ((low_16, ALU.bitwise_and, LO - 1), (high_16, ALU.arith_shift_right, LO.bit_length() - 1)):
                V.tensor_scalar(scratch, destinations, value, None, op)
                dve.drain()
                V.tensor_copy(part, scratch)
                dve.drain()

            def degree_hots(b, i, chunks=BC):
                for c in range(chunks):
                    slot = hot_deg[(BC * i + c) % 2]
                    hold(dve, deg_used, BC * b + c + 1)
                    for part, first, count in ((low_16, 0, LO), (high_16, LO, HI)):
                        V.tensor_tensor(slot[:, first:first + count, :],
                                        part[:, bass.ds((BC * b + c) * UT, UT)].unsqueeze(1).to_broadcast([P, count, UT]),
                                        iota_t[:, 0:count, :], ALU.is_equal).then_inc(deg_hot, 1)

            dve.wait_ge(consts, 1)
            for i in range(2):
                dve.sem_inc(x_free[0][i], 1)
            dve.wait_ge(x_in[0][0], 16)
            layer_norm(0, 0, 0, lambda c: xb[0][:, c, :])
            with dve.Fori(0, NPAIR - 1) as r:
                for i in range(2):
                    hold(dve, x_in[0][1 - i], 16 * r + 16 * (1 + i))
                    layer_norm(0, 1 - i, r + i, lambda c: xb[1 - i][:, c, :])
                    degree_hots(2 * r + i, i)
            for i in range(2):
                if i == 0:
                    dve.wait_ge(x_in[0][1], 16 * NPAIR)
                    layer_norm(0, 1, NPAIR - 1, lambda c: xb[1][:, c, :])
                degree_hots(2 * NPAIR - 2 + i, i, min(BC, UNITS - BC * (2 * NPAIR - 2 + i)))
            dve.wait_ge(deg_used, UNITS + 2)
            V.tensor_scalar(deg_few[:, :], bank[6][0:HI, 0:LO], 1.0, None, ALU.add).then_inc(deg_ready, 1)
            dve.wait_ge(sqrt_out, 1)
            V.reciprocal(deg_few[:, :], deg_few[:, :])
            dve.drain().then_inc(dinv_ready, 1)
            V.tensor_copy(dst_f[:, :, :], dst_i[:, :, :])
            dve.wait_ge(src_in, 32)
            scratch = key[:, 0:NA, :].bitcast(I32)
            V.tensor_scalar(scratch, src_i[:, 0:NA, :], P - 1, None, ALU.bitwise_and)
            dve.drain()
            V.tensor_scalar(src_lo[:, 0:NA, :], scratch, 1.0, None, ALU.add)
            V.memset(src_lo[:, NA, :], 0.0)
            dve.drain()
            V.tensor_scalar(scratch, src_i[:, 0:NA, :], P.bit_length() - 1, None, ALU.arith_shift_right)
            V.tensor_reduce(base0[:, :], dst_f[:, :, :], AX, ALU.min)
            V.tensor_reduce(span_in[:, NG:2 * NG], dst_f[:, :, :], AX, ALU.max)
            dve.drain()
            V.tensor_scalar(src_hi, scratch, float(WA), None, ALU.mult)
            V.tensor_scalar(span_in[:, 0:NG], base0[:, :], -1.0, None, ALU.mult)
            dve.drain().then_inc(span_ready, 1)
            dve.wait_ge(span_reduced, 1)
            V.tensor_scalar(base0[:, :], span[:, 0:NG], -1.0, None, ALU.mult)
            V.tensor_tensor(base_f[:, :], span[:, 0:NG], span[:, NG:2 * NG], ALU.add)
            dve.drain()
            V.tensor_reduce(widest[:, 0:1], base_f[:, 0:NA], AX, ALU.max)
            V.tensor_reduce(widest[:, 1:2], base_f[:, NA:NG], AX, ALU.max)
            dve.drain()
            for k, w in ((0, WA), (1, WB)):
                V.tensor_scalar(widest[:, k:k + 1], widest[:, k:k + 1], float(w), None, ALU.add)
            dve.drain()
            for k, w in ((0, WA), (1, WB)):
                V.tensor_scalar(reached[:, k, :], iota_1[:, 0:MOST], float(w), widest[:, k:k + 1], ALU.mult, ALU.is_le)
            dve.drain()
            V.tensor_reduce(widest[:, 0:2], reached[:, :, :], AX, ALU.add)
            dve.drain()
            V.tensor_reduce(widest[:, 2:3], widest[:, 0:2], AX, ALU.max)
            dve.drain()
            V.tensor_copy(passes_i[:, :], widest[:, 2:3])
            dve.drain().then_inc(passes_ready, 1)
            passes = dve.value_load(passes_i[0:1, 0:1], min_val=1, max_val=MOST)

            def first_windows():
                V.tensor_copy(base_f[:, :], base0[:, :])
                V.tensor_copy(base_i[:, :], base0[:, :])
                dve.drain()

            def next_windows():
                dve.drain()
                for c, w in ((slice(0, NA), WA), (slice(NA, NG), WB)):
                    V.tensor_scalar(base_f[:, c], base_f[:, c], float(w), float(NCAP), ALU.add, ALU.min)
                dve.drain()
                V.tensor_copy(base_i[:, :], base_f[:, :])
                dve.drain()

            def window_keys():
                V.scalar_tensor_tensor(key, dst_f, 1.0, base_f[:, :].unsqueeze(2).to_broadcast([P, NG, TE]), ALU.add, ALU.subtract)
                dve.drain()

            def pair_keys():
                k = key[:, 0:NA, :]
                V.tensor_scalar(in_win, k, float(WA), None, ALU.is_le)
                dve.drain()
                V.scalar_tensor_tensor(in_win, k, 1.0, in_win, ALU.is_ge, ALU.mult)
                V.tensor_tensor(k, k, src_hi, ALU.add)
                dve.drain()
                V.tensor_tensor(k, k, in_win, ALU.mult)
                dve.drain()

            def scale_and_split(l):
                S = NCB // TB
                if l == 0:
                    dve.sem_inc(tabT_read, 2)
                for b in range(S + 2):
                    if b < S:
                        c = slice(b * TB * P, min((b + 1) * TB * P, N))
                        V.tensor_tensor(feat[0:F, c], feat[0:F, c], dinv[:, c], ALU.mult)
                        if l:
                            dve.drain()
                            V.tensor_scalar(feat[0:F, c], feat[0:F, c], gb1c[:, :], 0.0, ALU.add, ALU.max)
                            dve.drain()
                            V.tensor_tensor(feat[0:F, c], feat[0:F, c], dinv[:, c], ALU.mult)
                        dve.drain().then_inc(scaled, 1)
                    if 1 <= b <= S:
                        m = b - 1
                        dve.wait_ge(high_ready, S * l + m + 1)
                        V.tensor_tensor(rest[m % 2], turned(m), parts[:, m * TB:(m + 1) * TB, 0, :], ALU.subtract)
                        dve.drain().then_inc(left_ready, 1)
                        dve.sem_inc(tabT_read, 1)
                    if b >= 2:
                        m = b - 2
                        dve.wait_ge(mid_ready, S * l + m + 1)
                        V.tensor_tensor(parts[:, m * TB:(m + 1) * TB, 2, :], rest[m % 2],
                                        parts[:, m * TB:(m + 1) * TB, 1, :], ALU.subtract)
                        dve.drain().then_inc(split, 1)

            def stage_keys(dest, source, g):
                V.tensor_copy(dest[:, :], source[:, bass.ds(g, 1), :].rearrange("p o t -> p (o t)"))

            def one_hot(out, keys, width):
                return V.tensor_tensor(out, keys[:, :].unsqueeze(2).to_broadcast([P, TE, width]),
                                       iota_1[:, 0:width].unsqueeze(1).to_broadcast([P, TE, width]), ALU.is_equal)

            def aggregate(l):
                L = layer[l]
                dve.sem_inc(L["acc_b"], 2)
                dve.sem_inc(L["summed"], 1)
                first_windows()
                with dve.Fori(0, passes) as j:
                    window_keys()
                    pair_keys()
                    stage_keys(lo_s[0], src_lo, 0)
                    stage_keys(key_s[0], key, 0)
                    dve.drain()
                    one_hot(hot_lo[0], lo_s[0], P)
                    for t in range(UR):
                        dve.wait_ge(L["used_a"], j * TILES_A + t + 1)
                        V.tensor_scalar(hot_key[t], iota_1[:, :], key_s[0][:, t:t + 1], None, ALU.is_equal).then_inc(L["hot_a"], 1)
                    with dve.Fori(0, STEPS // 2) as st:
                        turn = j * (STEPS // 2) + st

                        def hot_a(i, tiles):
                            if tiles[0] == 0:
                                stage_keys(lo_s[i % 2], src_lo, 2 * SA * st + i)
                                stage_keys(key_s[i % 2], key, 2 * SA * st + i)
                                dve.drain()
                                one_hot(hot_lo[i % 2], lo_s[i % 2], P)
                            for t in tiles:
                                dve.wait_ge(L["used_a"], st * (2 * SA * TE) + j * TILES_A + i * TE + t + 1)
                                V.tensor_scalar(hot_key[t % UR], iota_1[:, :], key_s[i % 2][:, t:t + 1], None, ALU.is_equal).then_inc(L["hot_a"], 1)

                        def hot_dst(i):
                            stage_keys(keyb_s[i % 2], key, NA + 2 * SB * st + i)
                            dve.drain()
                            one_hot(hot_b[i % 2], keyb_s[i % 2], WB).then_inc(L["hot_b"], 1)

                        def add_b(i):
                            b = dve.value_load(base_i[0:1, bass.ds(NA + 2 * SB * st + i, 1)], min_val=0, max_val=NCAP)
                            hold(dve, L["done_b"][i % 2], turn * SB + i // 2 + 2)
                            dve.drain()
                            V.tensor_tensor(feat[0:F, bass.ds(b, WB)], feat[0:F, bass.ds(b, WB)], bank[i % 2][0:F, 0:WB], ALU.add).then_inc(L["acc_b"], 1)

                        def add_a(half):
                            starts = [dve.value_load(base_i[0:1, bass.ds(2 * SA * st + half * SA + i, 1)], min_val=0, max_val=NCAP)
                                      for i in range(SA)]
                            hold(dve, L["product"], turn * 2 + half + 1)
                            for i, b in enumerate(starts):
                                dve.drain()
                                V.tensor_tensor(feat[0:F, bass.ds(b, WA)], feat[0:F, bass.ds(b, WA)],
                                                bank[6][0:F, i * WA:(i + 1) * WA], ALU.add)
                            dve.drain().then_inc(L["summed"], 1)

                        for half in range(2):
                            for i in range(SA):
                                hot_a(half * SA + i, range(UR, TE) if i == 0 else range(TE))
                                if i:
                                    add_b(half * SB + i - 1)
                                hot_dst(half * SB + i)
                            add_b(half * SB + SA - 1)
                            hot_dst(half * SB + SA)
                            hot_a((half + 1) * SA, range(UR))
                            add_a(half)
                            add_b(half * SB + SA)
                    next_windows()

            for k in range(2):
                dve.wait_ge(w_out[k], 16 * NE + 1)
            dve.wait_ge(dinv_in, 16)
            dve.wait_ge(norm[0]["mm_copied"], NCH)
            for l in range(2):
                V.memset(feat[0:F, N:AW], 0.0)
                if l:
                    dve.wait_ge(tab_stored[0], 16 * (NCB // TB))
                scale_and_split(l)
                aggregate(l)
            V.tensor_tensor(feat[0:F, 0:N], feat[0:F, 0:N], dinv[:, 0:N], ALU.mult)
            V.memset(feat[F:F + 1, 0:N], 1.0)
            dve.drain().then_inc(agg_done, 1)

            for i in range(2):
                dve.sem_inc(x_free[1][i], 1)
            dve.sem_inc(xnb_turned, 2)
            dve.sem_inc(xnb_kept, 2)
            with dve.Fori(0, NPAIR) as r:
                for i in range(2):
                    hold(dve, x_in[1][i], 16 * r + 16)
                    hold(dve, xnb_turned, 2 * r + i + 1)
                    hold(dve, xnb_kept, 2 * r + i + 1)
                    for c in range(BC):
                        hold(dve, z_ready, 2 * BC * r + BC * i + c + 2 * BC + 1)
                        V.scalar_tensor_tensor(xb[i][:, c, :], bank[4 + c % 4][0:CH, 0:D], 0.0, xb[i][:, c, :],
                                               ALU.max, ALU.add).then_inc(z_used, 1)
                    dve.drain().then_inc(norm[1]["x2_ready"], 1)
                    layer_norm(1, i, r, lambda c: xnb[i][:, c, :])
                    dve.sem_inc(x_free[1][i], 1)

            dve.wait_ge(norm[1]["mm_copied"], NCH)
            Q = slice(0, CH)
            V.tensor_tensor(logit[:, :, :], logit[:, :, :], bg_b[:, :].unsqueeze(1).to_broadcast([CH, NCH, NE]), ALU.add)
            V.memset(R["sel"][:, :, :], 0.0)
            dve.drain().then_inc(logits_done, 1)
            a, slot = R["a"], R["slot"]

            def over_e(v):
                return v.unsqueeze(2).to_broadcast([CH, NCH, NE])

            for k, mine in enumerate(("first", "second")):
                V.tensor_reduce(best[k][Q, :], logit[:, :, :], AX, ALU.max)
                dve.drain()
                V.tensor_tensor(a[Q], logit[:, :, :], over_e(best[k][Q, :]), ALU.is_equal)
                dve.drain()
                V.tensor_tensor(a[Q], a[Q], rev[Q, :].unsqueeze(1).to_broadcast([CH, NCH, NE]), ALU.mult)
                dve.drain()
                V.tensor_reduce(pick[Q, :], a[Q], AX, ALU.max)
                dve.drain()
                V.tensor_tensor(R[mine][Q], rev[Q, :].unsqueeze(1).to_broadcast([CH, NCH, NE]), over_e(pick[Q, :]), ALU.is_equal)
                dve.drain()
                if k == 0:
                    V.scalar_tensor_tensor(logit[:, :, :], R[mine][Q], -BIG, logit[:, :, :], ALU.mult, ALU.add)
                V.tensor_tensor(R["sel"][Q], R["sel"][Q], R[mine][Q], ALU.add)
                dve.drain()
            V.tensor_tensor(pick[Q, :], best[1][Q, :], best[0][Q, :], ALU.subtract)
            dve.drain().then_inc(sel_ready, 1)
            dve.wait_ge(exp_out, 1)
            V.tensor_scalar(prob[0][Q, :], prob[1][Q, :], 1.0, None, ALU.add)
            dve.drain()
            V.reciprocal(prob[0][Q, :], prob[0][Q, :])
            dve.drain()
            V.tensor_tensor(prob[1][Q, :], prob[1][Q, :], prob[0][Q, :], ALU.mult)
            dve.wait_ge(prefix_ready, 1)
            V.tensor_copy(sums[:, :, :].rearrange("p e c -> p c e"), bank[6][:, 0:NCH * NE].rearrange("p (c e) -> p c e", e=NE))
            dve.drain()
            V.tensor_tensor_scan(run[:, :, :].rearrange("p e c -> p (e c)"), ones_s[:, :],
                                 sums[:, :, :].rearrange("p e c -> p (e c)"), 0.0, ALU.mult, ALU.add)
            V.tensor_reduce(count[:, :], sums[:, :, :], AX, ALU.add)
            dve.drain()
            V.tensor_scalar(tiles_f[:, :], count[:, :], float(TS - 1), None, ALU.add)
            dve.drain()
            V.tensor_copy(tiles_i[:, :], tiles_f[:, :])
            dve.drain()
            V.tensor_scalar(tiles_i[:, :], tiles_i[:, :], SHIFT, None, ALU.arith_shift_right)
            dve.drain()
            V.tensor_copy(tiles_f[:, :], tiles_i[:, :])
            dve.drain()
            V.tensor_tensor_scan(tile_end[:, :], ones_s[:, 0:NE], tiles_f[:, :], 0.0, ALU.mult, ALU.add)
            V.tensor_tensor(offset[:, :], count[:, :], run[:, :, NCH - 1], ALU.subtract)
            dve.drain()
            V.tensor_tensor(tiles_f[:, :], tile_end[:, :], tiles_f[:, :], ALU.subtract)
            V.tensor_tensor(run[:, :, :], run[:, :, :], sums[:, :, :], ALU.subtract)
            V.tensor_scalar(widest[:, 0:1], tile_end[:, NE - 1:NE], 1.0, None, ALU.add)
            dve.drain()
            V.tensor_copy(pairs_i[:, :], widest[:, 0:1])
            dve.drain()
            V.tensor_scalar(pairs_i[:, :], pairs_i[:, :], 1, None, ALU.arith_shift_right)
            V.scalar_tensor_tensor(offset[:, :], tiles_f[:, :], float(TS), offset[:, :], ALU.mult, ALU.add)
            dve.drain()
            V.tensor_tensor(run[:, :, :], run[:, :, :], offset[:, :].unsqueeze(2).to_broadcast([P, NE, NCH]), ALU.add)
            dve.drain()
            V.tensor_tensor(slot[Q], run[Q, :, :].rearrange("p e c -> p c e"),
                            bank[7][Q, 0:NCH * NE].rearrange("p (c e) -> p c e", e=NE), ALU.add)
            V.tensor_tensor(passed[:, :, :], tile_no[:, :].unsqueeze(2).to_broadcast([P, NT + 1, NE]),
                            tile_end[:, :].unsqueeze(1).to_broadcast([P, NT + 1, NE]), ALU.is_ge)
            dve.drain()
            V.tensor_reduce(expert_f[:, :], passed[:, :, :], AX, ALU.add)
            dve.drain()
            V.tensor_scalar(expert_i[:, :], expert_f[:, :], float(NE - 1), None, ALU.min)
            for k, mine in enumerate(("first", "second")):
                V.tensor_tensor(a[Q], slot[Q], R[mine][Q], ALU.mult)
                dve.drain()
                V.tensor_reduce(pick[Q, :], a[Q], AX, ALU.add)
                dve.drain()
                V.tensor_copy(slot_i[k][Q, :], pick[Q, :])
                dve.drain()
            dve.drain().then_inc(routed, 1)

            dve.wait_ge(b2_in, 16)
            dve.sem_inc(y_copied, 2)
            for i in range(2):
                dve.sem_inc(y_stored[i], 1)
            dve_pairs = dve.value_load(pairs_i[0:1, 0:1], min_val=1, max_val=NTP)
            with dve.Fori(0, dve_pairs) as r:
                for i in range(2):
                    e = dve.value_load(expert_i[0:1, bass.ds(2 * r + i, 1)], min_val=0, max_val=NE - 1)
                    hold(dve, y_stored[i], 16 * r + 1)
                    hold(dve, y_ready, 2 * r + i + 1)
                    V.tensor_tensor(y[i][:, :, :], bank[6 + i][:, :].rearrange("p (h d) -> p h d", h=2),
                                    b2_b[:, bass.ds(e, 1), :].to_broadcast([P, 2, D]), ALU.add)
                    dve.drain().then_inc(y_copied, 1)

            for i in range(2):
                dve.sem_inc(out_stored[i], 1)
            with dve.Fori(0, NPAIR) as r:
                for i in range(2):
                    hold(dve, x2_in[i], 16 * r + 16)
                    hold(dve, y_gathered[i], (r + 1) * (32 * BC))
                    for k in range(2):
                        for c in range(BC):
                            V.scalar_tensor_tensor(comb[i][2][:, c, :], comb[i][k][:, c, :],
                                                   prob[k][Q, bass.ds((2 * r + i) * BC + c, 1)],
                                                   comb[i][2][:, c, :], ALU.mult, ALU.add)
                        dve.drain()
                    dve.drain().then_inc(combined, 1)

        @block.scalar
        def _(act):
            A = nc.scalar
            act.wait_ge(small_T, 1)
            A.copy(wgT[:, :, :].rearrange("p k e -> p (k e)"), bank[0][:, 0:DK * NE])
            A.copy(b1c[:, :], bank[1][:, 0:NE * HB])
            act.drain().then_inc(small_copied, 1)
            def std_out(s, b):
                hold(act, norm[s]["var_ready"], b + 1)
                A.activation(std[:, :], var[:, :], ACT.Sqrt).then_inc(norm[s]["std_ready"], 1)

            def turned_out(s, b, i, dest, between):
                q = norm[s]
                for c in range(BC + 1):
                    n = BC * i + c
                    if c < BC:
                        hold(act, q["xT_ready"], BC * b + c + 1)
                        A.copy(xT[n % 2][:, :, :].rearrange("p k c -> p (k c)"), bank[n % 2][:, 0:DK * CH]).then_inc(q["xT_copied"], 1)
                    if c:
                        hold(act, q["mm_ready"], BC * b + c)
                        dest((n - 1) % 2, BC * b + c - 1)
                    if c == (0, 2)[s] and between:
                        std_out(s, b + 1)

            def h_out(s, n):
                A.copy(feat[0:F, bass.ds(n * CH, CH)], bank[2 + s][0:F, 0:CH]).then_inc(norm[0]["mm_copied"], 1)

            def logit_out(s, n):
                A.copy(logit[:, bass.ds(n, 1), :].rearrange("p o e -> p (o e)"), bank[2 + s][0:CH, 0:NE]).then_inc(norm[1]["mm_copied"], 1)

            def first_block(b, i, between=True):
                turned_out(0, b, i, h_out, between)
                act.drain().then_inc(x_free[0][i], 1)

            def weights_out(e):
                for k, (stage, dram) in enumerate(((w1_out, w1t_d), (w2_out, w2t_d))):
                    hold(act, w_out[k], 16 * e + 1)
                    for n in range(4):
                        hold(act, w_T, 8 * e + 4 * k + n + 1)
                        A.copy(stage[:, n * 512:(n + 1) * 512], bank[4 + n % 2][:, :]).then_inc(w_evac, 1)
                    act.drain()
                    act.dma_start(dram[:, bass.ds(e, 1), :].rearrange("p o c -> p (o c)"), stage).then_inc(w_out[k], 16)

            act.sem_inc(w_evac, 2)
            for k in range(2):
                act.sem_inc(w_out[k], 1)
            std_out(0, 0)
            with act.Fori(0, NPAIR - 1) as r:
                for i in range(2):
                    first_block(2 * r + i, i)
                    weights_out(2 * r + i)
            first_block(2 * NPAIR - 2, 0)
            first_block(2 * NPAIR - 1, 1, between=False)

            act.wait_ge(deg_ready, 1)
            A.activation(deg_few[:, :], deg_few[:, :], ACT.Sqrt).then_inc(sqrt_out, 1)

            for k in range(2):
                act.wait_ge(w_out[k], 16 * NE + 1)

            def split_out(l):
                S = NCB // TB
                for b in range(S + 1):
                    if b < S:
                        act.wait_ge(tabT, S * l + b + 1)
                        A.copy(parts[:, b * TB:(b + 1) * TB, 0, :], turned(b)).then_inc(high_ready, 1)
                    if b:
                        m = b - 1
                        act.wait_ge(left_ready, S * l + m + 1)
                        A.copy(parts[:, m * TB:(m + 1) * TB, 1, :], rest[m % 2]).then_inc(mid_ready, 1)

            def counts_out(l):
                L = layer[l]
                act.sem_inc(L["evac"], len(PIECES))
                with act.Fori(0, act_passes) as j:
                    with act.Fori(0, STEPS) as st:
                        for i in range(SA):
                            b = 0
                            for k, nb in enumerate(PIECES):
                                hold(act, L["counted"], ((j * STEPS + st) * SA + i) * len(PIECES) + k + 1)
                                A.copy(counts[:, b:b + nb, i, :], bank[2 + k][:, 0:nb * WA].rearrange("p (b w) -> p b w", w=WA)).then_inc(L["evac"], 1)
                                b += nb

            act.wait_ge(passes_ready, 1)
            act_passes = act.value_load(passes_i[0:1, 0:1], min_val=1, max_val=MOST)
            for l in range(2):
                split_out(l)
                counts_out(l)
            act.wait_ge(agg_done, 1)
            act.sem_inc(z_ready, 2 * BC)

            def feat_out(b, i):
                hold(act, z_ready, BC * b + BC)
                A.copy(fblock[i], feat[:, bass.ds(b * (BC * CH), BC * CH)]).then_inc(f_copied, 1)

            def second_block(b, i, between=True):
                if between:
                    feat_out(b + 1, 1 - i)
                turned_out(1, b, i, logit_out, between)
                act.drain().then_inc(xnb_turned, 1)

            feat_out(0, 0)
            std_out(1, 0)
            with act.Fori(0, NPAIR - 1) as r:
                for i in range(2):
                    second_block(2 * r + i, i)
            second_block(2 * NPAIR - 2, 0)
            second_block(2 * NPAIR - 1, 1, between=False)
            act.wait_ge(sel_ready, 1)
            A.activation(prob[1][0:CH, :], pick[0:CH, :], ACT.Exp).then_inc(exp_out, 1)

            act.wait_ge(tokT_ready, 1)
            A.copy(tokT[0][:, :, :].rearrange("p k t -> p (k t)"), bank[0][:, :]).then_inc(tokT_copied, 1)
            act_pairs = act.value_load(pairs_i[0:1, 0:1], min_val=1, max_val=NTP)
            with act.Fori(0, act_pairs) as r:
                for i in range(2):
                    e = act.value_load(expert_i[0:1, bass.ds(2 * r + i, 1)], min_val=0, max_val=NE - 1)
                    for b in range(HB):
                        if b % 2 == 0:
                            hold(act, hid_ready, (2 * r + i) * (HB // 2) + b // 2 + 1)
                        A.activation(hid[:, b, :], bank[2 + b // 2][:, (b % 2) * TS:(b % 2 + 1) * TS], ACT.Relu,
                                     bias=b1c[:, bass.ds(e * HB + b, 1)]).then_inc(hid_copied, 1)
                    hold(act, tokT_ready, 2 * r + i + 2)
                    A.copy(tokT[1 - i][:, :, :].rearrange("p k t -> p (k t)"), bank[1 - i][:, :]).then_inc(tokT_copied, 1)

            with act.Fori(0, NPAIR) as r:
                for i in range(2):
                    hold(act, combined, 2 * r + i + 1)
                    act.dma_start(out_blk[bass.ds(2 * r + i, 1)].rearrange("o p c d -> (o p) c d"), comb[i][2]).then_inc(out_stored[i], 16)
            for i in range(2):
                act.wait_ge(out_stored[i], 16 * NPAIR + 1)

        @block.tensor
        def _(pe):
            T = nc.tensor
            pe.wait_ge(consts, 1)
            pe.wait_ge(weights_in, 112)
            for k in range(DK):
                T.transpose(bank[0][:, k * NE:(k + 1) * NE], wg_in[:, k * P:(k + 1) * P], ident[0:NE, 0:NE])
            T.transpose(bank[1][:, 0:NE * HB], b1_in[:, :], ident[0:NE * HB, 0:NE * HB])
            pe.drain().then_inc(small_T, 1)
            pe.wait_ge(small_copied, 1)
            def turn_block(s, b, i, source, product, beside=lambda c: None):
                q = norm[s]
                hold(pe, q["xn_ready"], b + 1)

                def turn(c):
                    for k in range(DK):
                        last = T.transpose(bank[(BC * i + c) % 2][:, k * CH:(k + 1) * CH], source[i][:, c, k * P:(k + 1) * P], ident[0:CH, 0:CH])
                    last.then_inc(q["xT_ready"], 1)

                turn(0)
                for c in range(BC):
                    if c + 1 < BC:
                        turn(c + 1)
                    hold(pe, q["xT_copied"], BC * b + c + 1)
                    product((BC * i + c) % 2).then_inc(q["mm_ready"], 1)
                    beside(c)

            def count_degrees(b, i, c, last_unit=False):
                hold(pe, deg_hot, 2 * (BC * b + c + 1))
                slot = hot_deg[(BC * i + c) % 2]
                for t in range(UT):
                    last = T.matmul(bank[6][0:HI, 0:LO], slot[:, LO:LO + HI, t], slot[:, 0:LO, t], start=False, stop=last_unit and t == UT - 1)
                last.then_inc(deg_used, 1)

            def h_product(slot):
                for k in range(DK):
                    last = T.matmul(bank[2 + slot][0:F, 0:CH], gw1[:, k, :], xT[slot][:, k, :], start=k == 0, stop=k == DK - 1)
                return last

            def turn_weights(e):
                for k in range(2):
                    hold(pe, w_in[k], 16 * e + 16)
                    for n in range(4):
                        hold(pe, w_evac, 8 * e + 4 * k + n + 1)
                        for m in range(4):
                            if k == 0:
                                q, b = n // 2, 4 * (n % 2) + m
                                block_in = w1_in[:, b, q * P:(q + 1) * P]
                            else:
                                q, b = (4 * n + m) % DK, (4 * n + m) // DK
                                block_in = w2_in[:, q, b * P:(b + 1) * P]
                            last = T.transpose(bank[4 + n % 2][:, m * P:(m + 1) * P], block_in, ident[:, :])
                        last.then_inc(w_T, 1)
                    pe.drain().then_inc(w_used[k], 1)

            pe.sem_inc(deg_used, 2)
            pe.wait_ge(zero_set, 1)
            T.matmul(bank[6][0:HI, 0:LO], zeros.bitcast(BF16)[:, 0:HI], ones_bf[:, 0:LO], start=True, stop=False)
            with pe.Fori(0, NPAIR - 1) as r:
                for i in range(2):
                    turn_block(0, 2 * r + i, i, xb, h_product, lambda c: count_degrees(2 * r + i, i, c))
                    turn_weights(2 * r + i)
            for i in range(2):
                b = 2 * NPAIR - 2 + i
                turn_block(0, b, i, xb, h_product, lambda c: count_degrees(b, i, c, BC * b + c == UNITS - 1) if BC * b + c < UNITS else None)
            pe.wait_ge(w_evac, 8 * NE + 2)
            pe.wait_ge(norm[0]["mm_copied"], NCH)

            pe.wait_ge(passes_ready, 1)
            passes = pe.value_load(passes_i[0:1, 0:1], min_val=1, max_val=MOST)

            def table_turn(l):
                for b in range(NCB // TB):
                    pe.wait_ge(scaled, (NCB // TB) * l + b + 1)
                    pe.wait_ge(tabT_read, (NCB // TB) * l + b + 1)
                    for c in range(TB):
                        last = T.transpose(bank[2 + b % 2][:, c * F:(c + 1) * F],
                                           feat[0:F, (TB * b + c) * P:(TB * b + c + 1) * P], ident[0:F, 0:F])
                    last.then_inc(tabT, 1)
                pe.wait_ge(split, (NCB // TB) * (l + 1))

            def aggregate(l):
                L = layer[l]
                pe.sem_inc(L["used_a"], UR)
                for i in range(2):
                    pe.sem_inc(L["done_b"][i], 1)
                with pe.Fori(0, passes) as j:
                    hold(pe, L["gathered_reset"], j + 1)
                    with pe.Fori(0, STEPS // 2) as st:
                        turn = j * (STEPS // 2) + st

                        def count_a(i):
                            for t in range(TE):
                                hold(pe, L["hot_a"], j * TILES_A + st * (2 * SA * TE) + i * TE + t + 1)
                                b = 0
                                for k, nb in enumerate(PIECES):
                                    if t == 0:
                                        hold(pe, L["evac"], turn * (2 * SA * len(PIECES)) + i * len(PIECES) + k + 1)
                                    mm = T.matmul(bank[2 + k][:, 0:nb * WA], hot_lo[i % 2][:, t, :], hot_key[t % UR][:, b * WA:(b + nb) * WA],
                                                  start=t == 0, stop=t == TE - 1)
                                    b += nb
                                    if t == TE - 1:
                                        mm.then_inc(L["counted"], 1)
                                if t < TE - 1:
                                    mm.then_inc(L["used_a"], 1)
                            pe.drain().then_inc(L["used_a"], 1)

                        def sum_b(i):
                            s = i % 2
                            hold(pe, L["hot_b"], turn * (2 * SB) + i + 1)
                            hold(pe, L["acc_b"], turn * (2 * SB) + i + 1)
                            hold(pe, L["gathered"][s], (st * SB + i // 2 + 1) * (16 * TE))
                            for t in range(TE):
                                for k in range(3):
                                    last = T.matmul(bank[s][0:F, 0:WB], rows[s][:, t, k, :], hot_b[s][:, t, :],
                                                    start=t == 0 and k == 0, stop=t == TE - 1 and k == 2)
                            last.then_inc(L["done_b"][s], 1)

                        def product(half):
                            hold(pe, L["evac"], (turn * 2 + half + 1) * (SA * len(PIECES)) + len(PIECES))
                            hold(pe, L["summed"], turn * 2 + half + 1)
                            for b in range(NCB):
                                for k in range(3):
                                    last = T.matmul(bank[6][0:F, 0:SA * WA], parts[:, b, k, :],
                                                    counts[:, b, :, :].rearrange("p i w -> p (i w)"),
                                                    start=b == 0 and k == 0, stop=b == NCB - 1 and k == 2)
                            last.then_inc(L["product"], 1)

                        for half in range(2):
                            for i in range(SA):
                                count_a(half * SA + i)
                                sum_b(half * SB + i)
                            product(half)
                            sum_b(half * SB + SA)
                    hold(pe, L["hot_a"], (j + 1) * TILES_A)
                    pe.sem_inc(L["used_a"], UR)

            for l in range(2):
                table_turn(l)
                aggregate(l)

            pe.wait_ge(agg_done, 1)
            pe.sem_inc(z_used, 1)

            def z_block(b, i):
                hold(pe, f_copied, b + 1)
                hold(pe, z_used, BC * b + 1)
                for c in range(BC):
                    if c >= 4:
                        hold(pe, z_used, BC * b + c - 2)
                    T.matmul(bank[4 + c % 4][0:CH, 0:D], fblock[i][:, c * CH:(c + 1) * CH], gw2[:, :], start=True, stop=True).then_inc(z_ready, 1)

            def gate_product(slot):
                for k in range(DK):
                    last = T.matmul(bank[2 + slot][0:CH, 0:NE], xT[slot][:, k, :], wgT[:, k, :], start=k == 0, stop=k == DK - 1)
                return last

            def second_block(b, i, ahead=True):
                if ahead:
                    z_block(b + 1, 1 - i)
                turn_block(1, b, i, xnb, gate_product)

            z_block(0, 0)
            with pe.Fori(0, NPAIR - 1) as r:
                for i in range(2):
                    second_block(2 * r + i, i)
            second_block(2 * NPAIR - 2, 0)
            second_block(2 * NPAIR - 1, 1, ahead=False)

            pe.wait_ge(sel_ready, 1)
            sel = R["sel"][0:CH].rearrange("p c e -> p (c e)")
            T.matmul(bank[6][:, 0:NCH * NE], ones_s[0:CH, 0:P], sel, start=True, stop=True)
            T.matmul(bank[7][0:CH, 0:NCH * NE], below[0:CH, 0:CH], sel, start=True, stop=True).then_inc(prefix_ready, 1)

            def turn_tokens(i):
                for h in range(2):
                    for k in range(DK):
                        last = T.transpose(bank[i][:, k * TS + h * P:k * TS + (h + 1) * P], tok[i][:, h, k * P:(k + 1) * P], ident[:, :])
                last.then_inc(tokT_ready, 1)

            pe.wait_ge(routed, 1)
            pe.wait_ge(wt_loaded, 16)
            pe.wait_ge(tok_in[0], 16)
            turn_tokens(0)
            pe_pairs = pe.value_load(pairs_i[0:1, 0:1], min_val=1, max_val=NTP)
            with pe.Fori(0, pe_pairs) as r:
                for i in range(2):
                    e = pe.value_load(expert_i[0:1, bass.ds(2 * r + i, 1)], min_val=0, max_val=NE - 1)
                    hold(pe, tokT_copied, 2 * r + i + 1)
                    hold(pe, w1_loaded[i], 16 * r + 16)
                    for b in range(HB):
                        for k in range(DK):
                            last = T.matmul(bank[2 + b // 2][:, (b % 2) * TS:(b % 2 + 1) * TS],
                                            w1t[i][:, k * H + b * P:k * H + (b + 1) * P], tokT[i][:, k, :],
                                            start=k == 0, stop=k == DK - 1)
                        if b % 2:
                            last.then_inc(hid_ready, 1)
                    hold(pe, tok_in[1 - i], 16 * r + 16 * (1 + i))
                    turn_tokens(1 - i)
                    hold(pe, y_copied, 2 * r + i + 1)
                    for h in range(2):
                        for b in range(HB):
                            if h == 0:
                                hold(pe, hid_copied, (2 * r + i) * HB + b + 1)
                            last = T.matmul(bank[6 + i][:, h * D:(h + 1) * D], hid[:, b, h * P:(h + 1) * P],
                                            w2t[:, bass.ds(e * (HB * D) + b * D, D)], start=b == 0, stop=b == HB - 1)
                    last.then_inc(y_ready, 1)


_INS = ['x', 'src', 'dst', 'L0_gnn_W1', 'L0_gnn_b1', 'L0_gnn_W2', 'L0_gnn_b2', 'L0_ffn_Wg', 'L0_ffn_bg',
        'L0_ffn_W1', 'L0_ffn_b1', 'L0_ffn_W2', 'L0_ffn_b2']


def kernel(**inputs):
    import numpy as np
    import concourse.bacc as bacc
    from concourse import mybir as mb
    from concourse.bass_utils import run_bass_kernel_spmd as run

    nc = bacc.Bacc("TRN2", target_bir_lowering=False, num_devices=1)
    arrays, args = {}, []
    for name in _INS:
        a = np.ascontiguousarray(inputs[name])
        arrays[f"in_{name}"] = a
        args.append(nc.dram_tensor(f"in_{name}", a.shape, mb.dt.from_np(a.dtype), kind="ExternalInput").ap())
    o = nc.dram_tensor("out_x", (N, D), mb.dt.float32, kind="ExternalOutput").ap()
    gnn_moe(nc, *args, o)
    r = run(nc, [arrays], core_ids=[0])
    return r.results[0]["out_x"]
```
